# Optimizing a Trainium2 kernel written in Bass

```python
import numpy as np
import jax
import jax.numpy as jnp

def _softmax(x, axis=-1):
    return jax.nn.softmax(x, axis=axis)

def _gelu(x):
    return jax.nn.gelu(x, approximate=True)

def _silu(x):
    return jax.nn.silu(x)

def _sigmoid(x):
    return jax.nn.sigmoid(x)

def _layernorm(x, axis=-1, eps=1e-05):
    m = jnp.mean(x, axis=axis, keepdims=True)
    v = jnp.var(x, axis=axis, keepdims=True)
    return (x - m) / jnp.sqrt(v + eps)

def _scatter_add(tgt, idx, src, axis=0):
    return tgt.at[idx].add(src)

def _segment_sum(src, seg, n):
    return jax.ops.segment_sum(src, seg, n)
kernel_name = 'mk_gnn_preln_d1_gnn_r8_38154a'

def setup_inputs(seed: int=0):
    np.random.seed(seed)
    _w = jnp.asarray

    def _rec_inputs():
        import jax
        import jax.numpy as jnp
        _gk = jax.random.key(seed)
        x = -0.0003713 + 1 * jax.random.normal(jax.random.fold_in(_gk, 1), (6250, 128), jnp.float32)
        src = jax.random.randint(jax.random.fold_in(_gk, 2), (200000,), 0, 6250, jnp.int32)
        dst = jnp.minimum((6250 * jax.random.uniform(jax.random.fold_in(_gk, 3), (200000,)) ** 2.0).astype(jnp.int32), 49999)
        _o = jnp.argsort(dst, stable=True)
        src = src[_o]
        dst = dst[_o]
        return (x, src, dst)
    x, src, dst = _rec_inputs()

    def _L0_gnn_setup():
        import jax, jax.numpy as jnp
        import numpy as np
        LN_EPS = 1e-05
        key = jax.random.key(seed)
        ks = jax.random.split(key, 6)
        N, E, D = (12500, 80000, 128)
        x = jax.random.normal(ks[0], (N, D), dtype=jnp.float32)
        edge_index = jax.random.randint(ks[1], (2, E), 0, N, dtype=jnp.int64)
        W_msg = jax.random.normal(ks[2], (D, D), dtype=jnp.float32) / np.sqrt(D)
        W_self = jax.random.normal(ks[3], (D, D), dtype=jnp.float32) / np.sqrt(D)
        b_self = jax.random.normal(ks[4], (D,), dtype=jnp.float32) * 0.02
        gamma = jnp.ones((D,), dtype=jnp.float32)
        beta = jnp.zeros((D,), dtype=jnp.float32)
        return {'x': x, 'edge_index': edge_index, 'W_msg': W_msg, 'W_self': W_self, 'b_self': b_self, 'gamma': gamma, 'beta': beta}
    _L0_gnn_all = _L0_gnn_setup()
    _L0_gnn_in = {k: v for k, v in _L0_gnn_all.items() if k in ('W_msg', 'W_self', 'b_self', 'gamma', 'beta')}
    del _L0_gnn_all
    return {'x': x, 'src': src, 'dst': dst, 'L0_gnn_W_msg': _L0_gnn_in['W_msg'], 'L0_gnn_W_self': _L0_gnn_in['W_self'], 'L0_gnn_b_self': _L0_gnn_in['b_self'], 'L0_gnn_gamma': _L0_gnn_in['gamma'], 'L0_gnn_beta': _L0_gnn_in['beta']}

def reference(x, src, dst, L0_gnn_W_msg, L0_gnn_W_self, L0_gnn_b_self, L0_gnn_gamma, L0_gnn_beta):
    import jax
    import jax.numpy as jnp

    def _L0_gnn_ref(x, edge_index, W_msg, W_self, b_self, gamma, beta):
        import jax, jax.numpy as jnp
        import numpy as np
        LN_EPS = 1e-05
        N = x.shape[0]
        src, dst = (edge_index[0], edge_index[1])
        msg = jnp.einsum('ed,fd->ef', x[src], W_msg)
        agg = jax.ops.segment_sum(msg, dst, num_segments=N)
        deg = jax.ops.segment_sum(jnp.ones_like(dst, dtype=x.dtype), dst, num_segments=N)
        agg = agg / jnp.maximum(deg, 1.0)[:, None]
        out = jnp.einsum('nd,fd->nf', x, W_self) + b_self + agg
        out = jax.nn.relu(out)
        mu = jnp.mean(out, axis=-1, keepdims=True)
        var = jnp.mean(jnp.square(out - mu), axis=-1, keepdims=True)
        return (out - mu) * jax.lax.rsqrt(var + LN_EPS) * gamma + beta
    edge_index = jnp.stack([src, dst])
    h = jnp.maximum(_layernorm(x, axis=-1), 0.0)
    x = x + _L0_gnn_ref(h, edge_index, L0_gnn_W_msg, L0_gnn_W_self, L0_gnn_b_self, L0_gnn_gamma, L0_gnn_beta)
    return x

_drawn_inputs = setup_inputs


def setup_inputs(seed=0):
    import zlib

    import numpy as np

    out = dict(_drawn_inputs(seed))
    spreads = {'L0_gnn_gamma': (1.0, 0.2), 'L0_gnn_beta': (0.0, 0.1)}
    factors = {}
    for name, (base, spread) in spreads.items():
        noise = np.random.default_rng([zlib.crc32(name.encode()), seed]).standard_normal(out[name].shape)
        drawn = base * np.exp(spread * noise) if base else spread * noise
        out[name] = jnp.asarray(drawn.astype(out[name].dtype))
    for name, factor in factors.items():
        out[name] = (out[name] * factor).astype(out[name].dtype)
    return out
```

```python
import numpy as np
import concourse.bass as bass
import concourse.mybir as mybir
from concourse.alu_op_type import AluOpType as ALU

ACT = mybir.ActivationFunctionType
F32 = mybir.dt.float32
F16 = mybir.dt.float16
I32 = mybir.dt.int32
U32 = mybir.dt.uint32

EPS = 1e-5
MAGIC = float(3 << 22)
HSCALE = 4096.0
SKIP = float(1 << 18)


def build_layer(nc, x, src, dst, w_msg, w_self, b_self, gamma, beta, out):
    N, D = x.shape
    E = src.shape[0]
    NP = 125
    NT = N // NP
    EC = 125
    NCH = E // EC
    WIN = 4
    NWIN = -(-N // WIN)
    G = 80
    NG = -(-(NCH + NWIN - 1) // G)
    NCOL = G * WIN
    MC = NT * WIN
    US = 4
    UPG = G // US
    RING = 4
    CP = 100
    CI = NCH // CP
    Q = 4
    RQ = NCOL // Q
    KQ = RQ // WIN
    BT = 10
    NB = NT // BT
    FREE_UNITS = 2
    assert NP * NT == N and EC * NCH == E and CP * CI == NCH and RQ * Q == NCOL and NG % 2 == 0 and BT * NB == NT
    assert MC * 2 <= 512 and UPG % RING == 0 and NCOL <= 512

    agg_rows = nc.dram_tensor("agg_rows", [N, D], F32, kind="Internal").ap()

    def sb(name, shape, dt):
        return nc.alloc_sbuf_tensor(name, shape, dt)

    def ps(name, shape, dt=F32):
        return nc.alloc_psum_tensor(name, shape, dt)

    def sem(name):
        return nc.alloc_semaphore(name)

    h_f32 = sb("h_f32", [NP, NT, D], F32)
    h_hi = sb("h_hi", [NP, NT, D], F16)
    h_lo = sb("h_lo", [NP, NT, D], F16)
    slab = sb("slab", [128, 2, NT, NCOL], F16)
    work = slab[:].rearrange("p b t c -> p (b t c)").bitcast(F32)
    x_in = work[0:NP, 0:NT * D].rearrange("p (t d) -> p t d", d=D)
    x_res = work[0:NP, 0:NT * D].rearrange("p (t d) -> p t d", d=D)
    agg_in = work[0:NP, NT * D:2 * NT * D].rearrange("p (t d) -> p t d", d=D)
    oh_part = sb("oh_part", [EC, RING, US, 128], F16)
    oh_cell = sb("oh_cell", [EC, RING, US, MC], F16)
    same_win = sb("same_win", [128, NG * G], F32)
    steps_bc = sb("steps_bc", [G, NG, G], F16)
    code_f = sb("code_f", [G, 8, EC], F32)
    codes = sb("codes", [G, 3, EC], F16)
    tabs = sb("tabs", [EC, 2, 3, G], F32)
    dst_rows = sb("dst_rows", [G, 2, EC], I32)
    src_rows = sb("src_rows", [G, 2, EC], I32)
    chunk_of = sb("chunk_of", [G, NG], U32)
    chunk_col = sb("chunk_col", [G, 2, 1], U32)
    slot_base = sb("slot_base", [G, NG], F32)
    slot_col = sb("slot_col", [G, 2, 1], F32)
    node_of = sb("node_of", [RQ, NG, Q], U32)
    node_col = sb("node_col", [RQ, 2, Q], U32)
    slot_oh = sb("slot_oh", [EC, WIN, G], F16)
    deg_scan = sb("deg_scan", [WIN, 2, G], F32)
    deg_diag = sb("deg_diag", [WIN, G, WIN], F32)
    deg_max = sb("deg_max", [RQ, Q], F32)
    deg_inv = sb("deg_inv", [RQ, NG, Q], F32)
    sums = sb("sums", [D, 2, NCOL], F32)
    rows = sb("rows", [RQ, 2, Q, D], F32)
    wm_t = sb("wm_t", [D, D], F32)
    ws_t = sb("ws_t", [D, D], F32)
    w_in = sb("w_in", [D, 2, D], F32)
    b_row = sb("b_row", [1, D], F32)
    gamma_bc = sb("gamma_bc", [NP, D], F32)
    beta_bc = sb("beta_bc", [NP, D], F32)
    zero_row = sb("zero_row", [NP, D], F32)
    stats = sb("stats", [NP, BT, 6], F32)
    mv = sb("mv", [NP, NT, 2], F32)
    rstd = sb("rstd", [NP, NT, 2], F32)
    h_t = sb("h_t", [D, 2, 4, NP], F32)
    diff = sb("diff", [128, 128], F32)
    ident = sb("ident", [128, 128], F32)
    ident16 = sb("ident16", [G, G], F16)
    tri_lt = sb("tri_lt", [CP, CP], F32)
    tri_le = sb("tri_le", [G, G], F32)
    ones = sb("ones", [128, 128], F32)
    ones16 = sb("ones16", [G, 128], F16)
    iota_part = sb("iota_part", [EC, 128], F16)
    iota_cell = sb("iota_cell", [EC, MC], F16)
    iota_g = sb("iota_g", [CP, G], F32)
    iota_slot = sb("iota_slot", [EC, WIN], F32)
    step_no = sb("step_no", [G, NG], F32)
    sel_src = sb("sel_src", [G, Q, RQ], F32)
    sel_here = sb("sel_here", [G, Q, RQ], F32)
    sel_next = sb("sel_next", [G, Q, RQ], F32)
    sel_wrap = sb("sel_wrap", [G, RQ], F32)
    slot_sel = sb("slot_sel", [EC, WIN, WIN], F16)
    slot_src = sb("slot_src", [EC, WIN, WIN], F32)
    row_slot = sb("row_slot", [RQ, 3], F32)
    ends = sb("ends", [CP, 3, CI], I32)
    ends_f = sb("ends_f", [CP, 3, CI], F32)
    wins = sb("wins", [CP, 3, CI], F32)
    n_steps = sb("n_steps", [CP, CI], F32)
    steps_inc = sb("steps_inc", [CP, CI], F32)
    steps_before = sb("steps_before", [CP, 1], F32)
    start = sb("start", [CP, CI], F32)
    start_gf = sb("start_gf", [CP, CI], F32)
    start_g = sb("start_g", [CP, CI], F32)
    start_k = sb("start_k", [CP, CI], F32)
    jump = sb("jump", [CP, CI], F32)
    oh_k = sb("oh_k", [CP, CI, G], F32)
    oh_g = sb("oh_g", [CP, CI, 2, NG], F32)
    marks = sb("marks", [G, 2, NG], F32)
    tot_scan = sb("tot_scan", [G, 2, NG], F32)
    tot_ex = sb("tot_ex", [G, 2, NG], F32)
    prefix = sb("prefix", [G, 2, NG], F32)
    window = sb("window", [G, NG], F32)
    cont = sb("cont", [G, NG], F32)
    cont_skip = sb("cont_skip", [G, NG + 1], F32)

    p_cnt = ps("p_cnt", [128, 2, 2, 512])
    p_main = ps("p_main", [128, 2, 512])
    p_misc = ps("p_misc", [128, 512])
    p_rows = ps("p_rows", [128, Q, D])
    p_tabs = p_misc[0:EC, 0:128].bitcast(F16)[:, 0:3 * G].rearrange("p (c k) -> p c k", c=3)
    p_deg = p_misc[0:WIN, 128:128 + G]
    p_degr = p_misc[0:RQ, 256:256 + Q]

    def tree(t):
        return t

    x_landed = [sem(f"x_landed{b}") for b in range(NB)]
    w_landed = sem("w_landed")
    ends_landed = sem("ends_landed")
    zeroed = sem("zeroed")
    zero_ready = sem("zero_ready")
    ends_set = sem("ends_set")
    iotas = sem("iotas")
    dve = sem("dve")
    consts_ready = sem("consts_ready")
    mv_ready = sem("mv_ready")
    std_ready = sem("std_ready")
    y_ready = sem("y_ready")
    relu_ready = sem("relu_ready")
    hi_ready = sem("hi_ready")
    lo_ready = sem("lo_ready")
    w_turned = sem("w_turned")
    w_ready = sem("w_ready")
    h_turned = sem("h_turned")
    ht_ready = sem("ht_ready")
    self_mm = sem("self_mm")
    self_ready = sem("self_ready")
    inc_ready = sem("inc_ready")
    before_mm = sem("before_mm")
    oh_steps = sem("oh_steps")
    marks_mm = sem("marks_mm")
    marks_ready = sem("marks_ready")
    prefix_mm = sem("prefix_mm")
    chunks_ready = sem("chunks_ready")
    windows_ready = sem("windows_ready")
    nodes_mm = sem("nodes_mm")
    nodes_ready = sem("nodes_ready")
    bc_ready = sem("bc_ready")
    bc_mm = sem("bc_mm")
    bc_out = sem("bc_out")
    gathered = [sem("gathered0"), sem("gathered1")]
    col_copied = sem("col_copied")
    pool_waits = sem("pool_waits")
    pool = sem("pool")
    codes_ready = sem("codes_ready")
    tabs_mm = sem("tabs_mm")
    tabs_ready = sem("tabs_ready")
    onehots_ready = sem("onehots_ready")
    counts_mm = sem("counts_mm")
    slab_written = sem("slab_written")
    main_mm = sem("main_mm")
    sums_ready = sem("sums_ready")
    slot_ready = sem("slot_ready")
    deg_mm = sem("deg_mm")
    deg_scanned = sem("deg_scanned")
    diag_ready = sem("diag_ready")
    degr_mm = sem("degr_mm")
    deg_max_done = sem("deg_max_done")
    deg_ready = sem("deg_ready")
    rows_mm = sem("rows_mm")
    rows_ready = sem("rows_ready")
    node_copied = sem("node_copied")
    scattered = [sem("scattered0"), sem("scattered1")]
    x_back = sem("x_back")
    agg_landed = [sem(f"agg_landed{b}") for b in range(NB)]
    xb_ready = sem("xb_ready")
    o_ready = sem("o_ready")
    o_relu = sem("o_relu")
    mv2_ready = sem("mv2_ready")
    std2_ready = sem("std2_ready")
    n_ready = sem("n_ready")
    gam_ready = sem("gam_ready")
    out_ready = sem("out_ready")
    stored = sem("stored")

    x_nodes = x.rearrange("(p t) d -> p t d", t=NT)
    out_nodes = out.rearrange("(p t) d -> p t d", t=NT)
    agg_nodes = agg_rows.rearrange("(p t) d -> p t d", t=NT)
    dst_chunks = dst.rearrange("(c e) -> c e", e=EC)
    src_chunks = src.rearrange("(c e) -> c e", e=EC)
    dst_ends = dst.rearrange("(p i e) -> p i e", i=CI, e=EC)

    self_batches = [(t, min(4, NT - t)) for t in range(0, NT, 4)]
    NBC = 400
    BCS = NG * G // NBC

    def in_groups(group, first, last):
        return group

    with nc.Block() as block:

        @block.sync
        def _(sp):
            with nc.allow_non_contiguous_dma(reason="one destination per chunk end"):
                sp.dma_start(ends[:, 0, :], dst_ends[:, :, 0]).then_inc(ends_landed, 16)
                sp.dma_start(ends[:, 1, :], dst_ends[:, :, EC - 1]).then_inc(ends_landed, 16)
                sp.dma_start(ends[:, 2, 1:CI], dst_ends[:, 0:CI - 1, EC - 1]).then_inc(ends_landed, 16)
                sp.dma_start(ends[1:CP, 2, 0:1], dst_ends[0:CP - 1, CI - 1:CI, EC - 1]).then_inc(ends_landed, 16)
            for b in range(NB):
                sp.dma_start(x_in[:, b * BT:(b + 1) * BT, :], x_nodes[:, b * BT:(b + 1) * BT, :]).then_inc(x_landed[b], 16)
            sp.dma_start(w_in[:, 0, :], w_msg).then_inc(w_landed, 16)
            sp.dma_start(w_in[:, 1, :], w_self).then_inc(w_landed, 16)
            sp.dma_start(b_row[:, :], b_self.rearrange("(a d) -> a d", a=1)).then_inc(w_landed, 16)
            sp.dma_start(gamma_bc[:, :], gamma.rearrange("(a d) -> a d", a=1).to_broadcast([NP, D])).then_inc(w_landed, 16)
            sp.dma_start(beta_bc[:, :], beta.rearrange("(a d) -> a d", a=1).to_broadcast([NP, D])).then_inc(w_landed, 16)
            sp.wait_ge(zero_ready, 1)
            sp.dma_start(agg_nodes, zero_row[:, :].unsqueeze(1).to_broadcast([NP, NT, D])).then_inc(zeroed, 16)
            sp.wait_ge(main_mm, NG)
            sp.dma_start(x_res, x_nodes).then_inc(x_back, 16)
            sp.wait_ge(scattered[0], 16 * Q * NG // 2)
            sp.wait_ge(scattered[1], 16 * Q * NG // 2)
            for b in range(NB):
                t = slice(b * BT, (b + 1) * BT)
                sp.dma_start(agg_in[:, t, :], agg_nodes[:, t, :]).then_inc(agg_landed[b], 16)
            for b in range(NB):
                t = slice(b * BT, (b + 1) * BT)
                sp.wait_ge(out_ready, b + 1)
                sp.dma_start(out_nodes[:, t, :], agg_in[:, t, :]).then_inc(stored, 16)
            sp.wait_ge(stored, 16 * NB)

        @block.gpsimd
        def _(gp):
            nc.gpsimd.memset(ends[0:1, 2, 0:1], -WIN).then_inc(ends_set, 1)
            nc.gpsimd.memset(zero_row[:, :], 0.0).then_inc(zero_ready, 1)
            nc.gpsimd.iota(diff[:, :], [[-1, 128]], base=0, channel_multiplier=1, allow_small_or_imprecise_dtypes=True).then_inc(iotas, 1)
            nc.gpsimd.iota(iota_g[:, :], [[1, G]], base=0, channel_multiplier=0, allow_small_or_imprecise_dtypes=True).then_inc(iotas, 1)
            nc.gpsimd.iota(step_no[:, :], [[G, NG]], base=0, channel_multiplier=1, allow_small_or_imprecise_dtypes=True).then_inc(iotas, 1)
            nc.gpsimd.iota(sel_src[:, :, :], [[-KQ, Q], [-1, KQ], [0, WIN]], base=0, channel_multiplier=1, allow_small_or_imprecise_dtypes=True).then_inc(iotas, 1)
            nc.gpsimd.iota(sel_wrap[:, :], [[-1, KQ], [0, WIN]], base=KQ - 1, channel_multiplier=1, allow_small_or_imprecise_dtypes=True).then_inc(iotas, 1)
            nc.gpsimd.iota(slot_src[:, :, :], [[1, WIN], [-1, WIN]], base=0, channel_multiplier=0, allow_small_or_imprecise_dtypes=True).then_inc(iotas, 1)
            nc.gpsimd.iota(iota_part[:, :], [[1, 128]], base=0, channel_multiplier=0, allow_small_or_imprecise_dtypes=True).then_inc(iotas, 1)
            nc.gpsimd.iota(iota_cell[:, :], [[1, MC]], base=1, channel_multiplier=0, allow_small_or_imprecise_dtypes=True).then_inc(iotas, 1)
            nc.gpsimd.iota(iota_slot[:, :], [[1, WIN]], base=1, channel_multiplier=0, allow_small_or_imprecise_dtypes=True).then_inc(iotas, 1)

            order = [0, 0, 0]

            def await_count(sem, value):
                gp.wait_ge(sem, value)
                gp.sem_inc(pool_waits, 1)

            def gather(g, par, i):
                await_count(col_copied, i)
                for rows_t, chunks in ((dst_rows, dst_chunks), (src_rows, src_chunks)):
                    gp.indirect_dma_start(out=rows_t[:, par, :], out_offset=None, in_=chunks,
                                          in_offset=bass.IndirectOffsetOnAxis(ap=chunk_col[:, par, :], axis=0),
                                          bounds_check=NCH - 1, oob_is_err=False).then_inc(gathered[par], 16)

            def copy_cols(par, col):
                gp.tensor_copy(chunk_col[:, par, :], chunk_of[:, col]).then_inc(col_copied, 1)

            NOPS = 11

            def make_codes(par, col, n_gathered, p0, n_turned):
                slot, off, far, part_f, part, four, rest, cell = (code_f[:, j, :] for j in range(8))
                gp.tensor_copy(slot_col[:, par, :], slot_base[:, col]).then_inc(pool, 1)
                await_count(gathered[par], n_gathered)
                await_count(pool, p0 + 1)
                gp.tensor_scalar(slot, dst_rows[:, par, :], slot_col[:, par, :], None, ALU.subtract).then_inc(pool, 1)
                gp.tensor_scalar(part_f, src_rows[:, par, :], (NT - 1) / 2.0, 1.0 / NT, ALU.subtract, ALU.mult).then_inc(pool, 1)
                gp.tensor_scalar(four, src_rows[:, par, :], float(WIN), None, ALU.mult).then_inc(pool, 1)
                await_count(pool, p0 + 4)
                gp.tensor_scalar(off, slot, -(WIN + 1) / 2.0, None, ALU.add).then_inc(pool, 1)
                gp.tensor_scalar(part, part_f, MAGIC, MAGIC, ALU.add, ALU.subtract).then_inc(pool, 1)
                gp.tensor_tensor(four, four, slot, ALU.add).then_inc(pool, 1)
                await_count(pool, p0 + 7)
                gp.tensor_tensor(off, off, off, ALU.mult).then_inc(pool, 1)
                gp.tensor_scalar(rest, part, -float(NT * WIN), None, ALU.mult).then_inc(pool, 1)
                await_count(pool, p0 + 9)
                gp.tensor_scalar(far, off, WIN * WIN / 4.0, 16384.0, ALU.is_gt, ALU.mult).then_inc(pool, 1)
                await_count(pool, p0 + 10)
                gp.tensor_tensor(cell, four, far, ALU.add).then_inc(pool, 1)
                if n_turned is not None:
                    await_count(tabs_mm, n_turned)
                gp.tensor_copy(codes[:, 0, :], part).then_inc(codes_ready, 1)
                gp.tensor_copy(codes[:, 2, :], slot).then_inc(codes_ready, 1)
                await_count(pool, p0 + 11)
                gp.tensor_tensor(codes[:, 1, :], cell, rest, ALU.add).then_inc(codes_ready, 1)

            def diag(par, g1):
                await_count(deg_scanned, g1)
                await_count(degr_mm, g1 - 1)
                gp.tensor_tensor(deg_diag[:, :, :], deg_scan[:, par, :].unsqueeze(2).to_broadcast([WIN, G, WIN]),
                                 ident[0:WIN, 0:WIN].unsqueeze(1).to_broadcast([WIN, G, WIN]), ALU.mult).then_inc(diag_ready, 1)

            def scatter(par, col, n_rows, n_copied):
                if n_copied is not None:
                    await_count(scattered[par], n_copied)
                gp.tensor_copy(node_col[:, par, :], node_of[:, col, :]).then_inc(node_copied, 1)
                await_count(node_copied, n_rows)
                await_count(rows_ready, n_rows)
                for q in range(Q):
                    gp.indirect_dma_start(out=agg_rows, out_offset=bass.IndirectOffsetOnAxis(ap=node_col[:, par, q:q + 1], axis=0),
                                          in_=rows[:, par, q, :], in_offset=None,
                                          bounds_check=N - 1, oob_is_err=False).then_inc(scattered[par], 16)

            def group(g, i, par, fetch=True, code=True, deg=True, store=True, first_store=False):
                if fetch:
                    await_count(codes_ready, 3 * (g + 1))
                    copy_cols(par, one(g + 2))
                    gather(None, par, g + 3)
                if code:
                    par1 = 1 - par
                    make_codes(par1, one(g + 1), 32 * (i + 1 + par), NOPS * (g + 1), g + 1)
                if deg:
                    diag(par, g + 1)
                if store:
                    scatter(par, g - 2, g - 1, None if first_store else 16 * Q * (i - 1))

            def one(a):
                return bass.ds(a, 1)

            gp.wait_ge(chunks_ready, 1)
            copy_cols(0, slice(0, 1))
            copy_cols(1, slice(1, 2))
            gather(None, 0, 1)
            gather(None, 1, 2)
            gp.wait_ge(windows_ready, 1)
            make_codes(0, slice(0, 1), 32, 0, None)
            gp.wait_ge(nodes_ready, 1)
            gp.wait_ge(zeroed, 16)
            gp.wait_ge(consts_ready, 1)
            group(0, 0, 0, store=False)
            group(1, 0, 1, store=False)
            group(2, 1, 0, first_store=True)
            group(3, 1, 1, first_store=True)
            with gp.Fori(2, NG // 2 - 1) as i:
                group(2 * i, i, 0)
                group(2 * i + 1, i, 1)
            group(NG - 2, NG // 2 - 1, 0, fetch=False)
            group(NG - 1, NG // 2 - 1, 1, fetch=False, code=False)
            group(NG, NG // 2, 0, fetch=False, code=False, deg=False)
            group(NG + 1, NG // 2, 1, fetch=False, code=False, deg=False)

            gp.wait_ge(x_back, 16)
            gp.wait_ge(w_landed, 80)
            gp.tensor_tensor(x_res, x_res, beta_bc[:, :].unsqueeze(1).to_broadcast([NP, NT, D]), ALU.add).then_inc(xb_ready, 1)
            gp.wait_ge(xb_ready, 1)
            for b in range(NB):
                t = slice(b * BT, (b + 1) * BT)
                gp.wait_ge(n_ready, b + 1)
                gp.tensor_tensor(agg_in[:, t, :], agg_in[:, t, :], gamma_bc[:, :].unsqueeze(1).to_broadcast([NP, BT, D]), ALU.mult).then_inc(gam_ready, 1)
                gp.wait_ge(gam_ready, b + 1)
                gp.tensor_tensor(agg_in[:, t, :], agg_in[:, t, :], x_res[:, t, :], ALU.add).then_inc(out_ready, 1)

        def turn_codes(act, g, par=0):
            act.wait_ge(tabs_mm, g + 1)
            if not isinstance(g, int) or g >= 2:
                act.wait_ge(onehots_ready, UPG * (g - 1))
                act.wait_ge(slot_ready, g - 1)
            act.activation(tabs[:, par, :, :], p_tabs, ACT.Copy).then_inc(tabs_ready, 1)

        @block.scalar
        def _(act):
            for j in range(BCS):
                act.wait_ge(bc_mm, j + 1)
                act.activation(same_win[:, j * NBC:(j + 1) * NBC], p_cnt[:, (j // 2) % 2, j % 2, 0:NBC], ACT.Copy).then_inc(bc_out, 1)
            act.wait_ge(w_turned, 1)
            act.activation(wm_t[:, :], p_rows[:, 0, :], ACT.Copy, scale=1.0 / HSCALE).then_inc(w_ready, 1)
            act.activation(ws_t[:, :], p_rows[:, 1, :], ACT.Copy).then_inc(w_ready, 1)
            for b in range(NB):
                t = slice(b * BT, (b + 1) * BT)
                act.wait_ge(mv_ready, b + 1)
                act.activation(rstd[:, t, 0], mv[:, t, 1], ACT.Sqrt).then_inc(std_ready, 1)
                act.wait_ge(y_ready, b + 1)
                act.activation(h_f32[:, t, :], h_f32[:, t, :], ACT.Relu).then_inc(relu_ready, 1)
                act.wait_ge(relu_ready, b + 1)
                act.activation(h_hi[:, t, :], h_f32[:, t, :], ACT.Copy, scale=HSCALE).then_inc(hi_ready, 1)
            turn_codes(act, 0)
            for n, (t, k) in enumerate(self_batches):
                act.wait_ge(h_turned, n + 1)
                if n >= 2:
                    act.wait_ge(self_mm, n - 1)
                act.activation(h_t[:, n % 2, 0:k, :], p_main[:, n % 2, :].rearrange("p (t e) -> p t e", t=4)[:, 0:k, 0:NP], ACT.Copy).then_inc(ht_ready, 1)

            def group(g, par, counts=True, codes_next=True, has_rows=True, guard_rows=True):
                for u in range(UPG):
                    if counts:
                        act.wait_ge(counts_mm, UPG * g + u + 1)
                        if u == 0 and (not isinstance(g, int) or g >= 2):
                            act.wait_ge(main_mm, g - 1)
                        act.activation(
                            slab[:, par, :, u * US * WIN:(u + 1) * US * WIN].rearrange("p t (b c) -> p b t c", b=2),
                            p_cnt[:, u % 2, :, 0:2 * MC].rearrange("p b (t c) -> p b t c", c=2 * WIN),
                            ACT.Copy).then_inc(slab_written, 1)
                    if u == 6 and codes_next:
                        turn_codes(act, g + 1, 1 - par)
                    if u == 12 and has_rows:
                        act.wait_ge(rows_mm, g - 1)
                        act.wait_ge(deg_ready, g - 1)
                        if guard_rows:
                            act.wait_ge(scattered[par], 8 * Q * (g - par) - 16 * Q)
                        for q in range(Q):
                            last = act.activation(rows[:, par, q, :], p_rows[0:RQ, q, :], ACT.Copy, scale=deg_inv[:, g - 2, q:q + 1])
                        last.then_inc(rows_ready, 1)

            group(0, 0, has_rows=False)
            group(1, 1, has_rows=False)
            group(2, 0, guard_rows=False)
            group(3, 1, guard_rows=False)
            with act.Fori(2, NG // 2 - 1) as i:
                group(2 * i, 0)
                group(2 * i + 1, 1)
            group(NG - 2, 0)
            group(NG - 1, 1, codes_next=False)
            group(NG, 0, counts=False, codes_next=False)
            group(NG + 1, 1, counts=False, codes_next=False)

            for b in range(NB):
                t = slice(b * BT, (b + 1) * BT)
                act.wait_ge(o_ready, b + 1)
                act.activation(agg_in[:, t, :], agg_in[:, t, :], ACT.Relu).then_inc(o_relu, 1)
                act.wait_ge(mv2_ready, b + 1)
                act.activation(rstd[:, t, 0], mv[:, t, 1], ACT.Sqrt).then_inc(std2_ready, 1)

        @block.vector
        def _(v):
            done = [0]

            def own(ins):
                done[0] += 1
                ins.then_inc(dve, 1)
                v.wait_ge(dve, done[0])

            v.wait_ge(iotas, 9)
            v.tensor_scalar(ident[:, :], diff[:, :], 0.0, None, ALU.is_equal)
            v.tensor_scalar(ident16[:, :], diff[0:G, 0:G], 0.0, None, ALU.is_equal)
            v.tensor_scalar(tri_lt[:, :], diff[0:CP, 0:CP], 0.0, None, ALU.is_lt)
            v.tensor_scalar(tri_le[:, :], diff[0:G, 0:G], 0.0, None, ALU.is_le)
            v.tensor_scalar(sel_here[:, :, :], sel_src[:, :, :], 0.0, None, ALU.is_equal)
            v.tensor_scalar(sel_next[:, :, :], sel_src[:, :, :], 1.0, None, ALU.is_equal)
            v.tensor_scalar(slot_sel[:, :, :], slot_src[:, :, :], 0.0, None, ALU.is_equal)
            v.memset(ones[:, :], 1.0)
            v.memset(ones16[:, :], 1.0)
            own(v.memset(cont_skip[:, :], 0.0))
            own(v.tensor_scalar(sel_wrap[:, :], sel_wrap[:, :], 0.0, None, ALU.is_equal))
            own(v.tensor_scalar(row_slot[:, 0:1], diff[0:RQ, 0:1], (WIN - 1) / 2.0, 1.0 / WIN, ALU.subtract, ALU.mult))
            own(v.tensor_scalar(row_slot[:, 1:2], row_slot[:, 0:1], MAGIC, MAGIC, ALU.add, ALU.subtract))
            v.scalar_tensor_tensor(out=row_slot[:, 2:3], in0=row_slot[:, 1:2], scalar=-float(WIN), in1=diff[0:RQ, 0:1],
                                   op0=ALU.mult, op1=ALU.add).then_inc(consts_ready, 1)

            v.wait_ge(ends_landed, 64)
            v.wait_ge(ends_set, 1)
            own(v.tensor_scalar(ends_f[:, :, :], ends[:, :, :], (WIN - 1) / 2.0, 1.0 / WIN, ALU.subtract, ALU.mult))
            own(v.tensor_scalar(wins[:, :, :], ends_f[:, :, :], MAGIC, MAGIC, ALU.add, ALU.subtract))
            own(v.scalar_tensor_tensor(out=n_steps[:, :], in0=wins[:, 1, :], scalar=1.0, in1=wins[:, 0, :], op0=ALU.add, op1=ALU.subtract))
            v.tensor_tensor_scan(steps_inc[:, :], ones[0:CP, 0:CI], n_steps[:, :], 0.0, ALU.mult, ALU.add).then_inc(inc_ready, 1)
            v.scalar_tensor_tensor(out=jump[:, :], in0=wins[:, 0, :], scalar=-1.0, in1=wins[:, 2, :], op0=ALU.add, op1=ALU.subtract)
            v.wait_ge(before_mm, 1)
            own(v.tensor_copy(steps_before[:, :], p_misc[0:CP, 0:1]))
            own(v.scalar_tensor_tensor(out=start[:, :], in0=steps_inc[:, :], scalar=steps_before[:, :], in1=n_steps[:, :], op0=ALU.add, op1=ALU.subtract))
            own(v.tensor_scalar(start_gf[:, :], start[:, :], (G - 1) / 2.0, 1.0 / G, ALU.subtract, ALU.mult))
            own(v.tensor_scalar(start_g[:, :], start_gf[:, :], MAGIC, MAGIC, ALU.add, ALU.subtract))
            own(v.scalar_tensor_tensor(out=start_k[:, :], in0=start_g[:, :], scalar=-float(G), in1=start[:, :], op0=ALU.mult, op1=ALU.add))
            v.tensor_tensor(oh_k[:, :, :], iota_g[:, :].unsqueeze(1).to_broadcast([CP, CI, G]),
                            start_k[:, :].unsqueeze(2).to_broadcast([CP, CI, G]), ALU.is_equal)
            own(v.tensor_tensor(oh_g[:, :, 0, :], iota_g[:, 0:NG].unsqueeze(1).to_broadcast([CP, CI, NG]),
                                start_g[:, :].unsqueeze(2).to_broadcast([CP, CI, NG]), ALU.is_equal))
            v.tensor_tensor(oh_g[:, :, 1, :], oh_g[:, :, 0, :], jump[:, :].unsqueeze(2).to_broadcast([CP, CI, NG]), ALU.mult).then_inc(oh_steps, 1)
            v.wait_ge(marks_mm, 1)
            v.tensor_copy(marks[:, :, :], p_misc[0:G, 0:2 * NG].rearrange("p (h g) -> p h g", h=2)).then_inc(marks_ready, 1)
            v.wait_ge(marks_ready, 1)
            own(v.tensor_scalar(cont[:, :], marks[:, 1, :], -1.0, None, ALU.is_equal))
            v.tensor_tensor(steps_bc[:, :, :], ident16[:, :].unsqueeze(1).to_broadcast([G, NG, G]),
                            cont[:, :].unsqueeze(2).to_broadcast([G, NG, G]), ALU.mult).then_inc(bc_ready, 1)
            v.tensor_scalar(cont_skip[:, 0:NG], cont[:, :], SKIP, None, ALU.mult)
            v.wait_ge(prefix_mm, 1)
            totals = p_rows[0:G, 0, 0:2 * NG].rearrange("p (h g) -> p h g", h=2)
            within = p_rows[0:G, 1, 0:2 * NG].rearrange("p (h g) -> p h g", h=2)
            v.tensor_tensor_scan(tot_scan[:, 0, :], ones[0:G, 0:NG], totals[:, 0, :], 0.0, ALU.mult, ALU.add)
            own(v.tensor_tensor_scan(tot_scan[:, 1, :], ones[0:G, 0:NG], totals[:, 1, :], 0.0, ALU.mult, ALU.add))
            own(v.tensor_tensor(tot_ex[:, :, :], tot_scan[:, :, :], totals, ALU.subtract))
            own(v.tensor_tensor(prefix[:, :, :], tot_ex[:, :, :], within, ALU.add))
            v.tensor_scalar(chunk_of[:, :], prefix[:, 0, :], -1.0, None, ALU.add).then_inc(chunks_ready, 1)
            own(v.tensor_tensor(window[:, :], prefix[:, 1, :], step_no[:, :], ALU.add))
            v.tensor_scalar(slot_base[:, :], window[:, :], float(WIN), -1.0, ALU.mult, ALU.add).then_inc(windows_ready, 1)
            v.wait_ge(nodes_mm, 1)
            v.wait_ge(consts_ready, 1)
            v.tensor_scalar(node_of[:, :, :].rearrange("p g q -> p q g"), p_misc[0:RQ, 0:Q * NG].rearrange("p (q g) -> p q g", q=Q),
                            float(WIN), row_slot[:, 2:3], ALU.mult, ALU.add).then_inc(nodes_ready, 1)

            def tile_stats(src_t, t0, n_ready):
                for j in range(BT):
                    last = v.bn_stats(stats[:, j, :], src_t[:, t0 + j, :])
                own(last)
                for j in range(BT):
                    last = v.bn_aggr(mv[:, t0 + j, :], stats[:, j, :])
                own(last)
                v.tensor_scalar(mv[:, t0:t0 + BT, 1], mv[:, t0:t0 + BT, 1], EPS, None, ALU.add).then_inc(n_ready, 1)

            for b in range(NB):
                t0 = b * BT
                t = slice(t0, t0 + BT)
                v.wait_ge(x_landed[b], 16)
                tile_stats(x_in, t0, mv_ready)
                v.wait_ge(std_ready, b + 1)
                own(v.reciprocal(rstd[:, t, 1], rstd[:, t, 0]))
                for j in range(t0, t0 + BT):
                    last = v.tensor_scalar(h_f32[:, j, :], x_in[:, j, :], mv[:, j, 0:1], rstd[:, j, 1:2], ALU.subtract, ALU.mult)
                last.then_inc(y_ready, 1)
                v.wait_ge(hi_ready, b + 1)
                v.scalar_tensor_tensor(out=h_lo[:, t, :], in0=h_f32[:, t, :], scalar=HSCALE, in1=h_hi[:, t, :],
                                       op0=ALU.mult, op1=ALU.subtract).then_inc(lo_ready, 1)
            for n, (t, k) in enumerate(self_batches):
                v.wait_ge(self_mm, n + 1)
                v.tensor_copy(h_f32[:, t:t + k, :], p_cnt[0:NP, 1, n % 2, 0:k * D].rearrange("p (t d) -> p t d", d=D)).then_inc(self_ready, 1)

            def group(g, par, build=True, join=True, first_join=False, last_deg=True):
                if build:
                    v.wait_ge(tabs_ready, g + 1)
                for u in range(UPG):
                    r = u % RING
                    if build:
                        if not (isinstance(g, int) and g == 0 and u < RING):
                            v.wait_ge(counts_mm, UPG * g + u + 1 - RING)
                        for s in range(US):
                            k = u * US + s
                            v.tensor_scalar(oh_part[:, r, s, :], iota_part[:, :], tabs[:, par, 0, k:k + 1], None, ALU.is_equal)
                            last = v.tensor_scalar(oh_cell[:, r, s, :], iota_cell[:, :], tabs[:, par, 1, k:k + 1], None, ALU.is_equal)
                        last.then_inc(onehots_ready, 1)
                        if u == 0:
                            if not (isinstance(g, int) and g == 0):
                                v.wait_ge(deg_mm, g)
                            v.tensor_tensor(slot_oh[:, :, :], tabs[:, par, 2, :].unsqueeze(1).to_broadcast([EC, WIN, G]),
                                            iota_slot[:, :].unsqueeze(2).to_broadcast([EC, WIN, G]), ALU.is_equal).then_inc(slot_ready, 1)
                        if u == 13:
                            v.wait_ge(deg_mm, g + 1)
                            first = isinstance(g, int) and g == 0
                            if not first:
                                v.wait_ge(deg_scanned, g)
                                v.wait_ge(diag_ready, g)
                            v.tensor_tensor_scan(deg_scan[:, par, :], same_win[0:WIN, at(g)], p_deg,
                                                 0.0 if first else deg_scan[:, 1 - par, G - 1:G], ALU.mult, ALU.add).then_inc(deg_scanned, 1)
                    if u == 1 and last_deg:
                        v.wait_ge(degr_mm, g)
                        if not (isinstance(g, int) and g == 1):
                            v.wait_ge(deg_ready, g - 1)
                        v.tensor_scalar(deg_max[:, :], p_degr, 1.0, None, ALU.max).then_inc(deg_max_done, 1)
                        v.wait_ge(deg_max_done, g)
                        v.reciprocal(deg_inv[:, g - 1, :], deg_max[:, :]).then_inc(deg_ready, 1)
                    if u == 6 and join:
                        v.wait_ge(main_mm, g - 1)
                        if not first_join:
                            v.wait_ge(sums_ready, g - 2)
                            if not (isinstance(g, int) and g == 3):
                                v.wait_ge(rows_mm, g - 3)
                        for r4 in range(WIN):
                            last = v.tensor_tensor_scan(sums[:, par, r4:NCOL:WIN], same_win[:, at(g - 2)], p_main[:, par, r4:NCOL:WIN],
                                                        0.0 if first_join else sums[:, 1 - par, NCOL - WIN + r4:NCOL - WIN + r4 + 1],
                                                        ALU.mult, ALU.add)
                        last.then_inc(sums_ready, 1)

            def at(g):
                return bass.ds(g * G, G)

            group(0, 0, join=False, last_deg=False)
            group(1, 1, join=False)
            group(2, 0, first_join=True)
            group(3, 1)
            with v.Fori(2, NG // 2) as i:
                group(2 * i, 0)
                group(2 * i + 1, 1)
            group(NG, 0, build=False)
            group(NG + 1, 1, build=False, last_deg=False)

            for b in range(NB):
                t0 = b * BT
                t = slice(t0, t0 + BT)
                v.wait_ge(agg_landed[b], 16)
                v.wait_ge(self_ready, len(self_batches))
                v.tensor_tensor(agg_in[:, t, :], agg_in[:, t, :], h_f32[:, t, :], ALU.add).then_inc(o_ready, 1)
                v.wait_ge(o_relu, b + 1)
                tile_stats(agg_in, t0, mv2_ready)
                v.wait_ge(std2_ready, b + 1)
                own(v.reciprocal(rstd[:, t, 1], rstd[:, t, 0]))
                for j in range(t0, t0 + BT):
                    last = v.tensor_scalar(agg_in[:, j, :], agg_in[:, j, :], mv[:, j, 0:1], rstd[:, j, 1:2], ALU.subtract, ALU.mult)
                last.then_inc(n_ready, 1)

        @block.tensor
        def _(pe):
            pe.wait_ge(consts_ready, 1)
            pe.wait_ge(inc_ready, 1)
            pe.matmul(p_misc[0:CP, 0:1], tri_lt[:, :], steps_inc[:, CI - 1:CI], start=True, stop=True).then_inc(before_mm, 1)
            pe.wait_ge(w_landed, 80)
            pe.wait_ge(oh_steps, 1)
            for i in range(CI):
                mm = pe.matmul(p_misc[0:G, 0:2 * NG], oh_k[:, i, :], oh_g[:, i, :, :].rearrange("p h g -> p (h g)"),
                               start=(i == 0), stop=(i == CI - 1))
            mm.then_inc(marks_mm, 1)
            pe.wait_ge(marks_ready, 1)
            flat = marks[:, :, :].rearrange("p h g -> p (h g)")
            pe.matmul(p_rows[0:G, 0, 0:2 * NG], ones[0:G, 0:G], flat, start=True, stop=True)
            pe.matmul(p_rows[0:G, 1, 0:2 * NG], tri_le[:, :], flat, start=True, stop=True).then_inc(prefix_mm, 1)
            pe.wait_ge(bc_ready, 1)
            flat = steps_bc[:, :, :].rearrange("p g k -> p (g k)")
            for j in range(BCS):
                if j >= 4:
                    pe.wait_ge(bc_out, j - 3)
                pe.matmul(p_cnt[:, (j // 2) % 2, j % 2, 0:NBC], ones16[:, :], flat[:, j * NBC:(j + 1) * NBC], start=True, stop=True).then_inc(bc_mm, 1)
            pe.wait_ge(windows_ready, 1)
            for q in range(Q):
                o = p_misc[0:RQ, q * NG:(q + 1) * NG]
                pe.matmul(o, sel_here[:, q, :], window[:, :], start=True, stop=False)
                mm = pe.matmul(o, sel_next[:, q, :], cont_skip[:, 0:NG], start=False, stop=(q < Q - 1))
                if q == Q - 1:
                    mm = pe.matmul(o, sel_wrap[:, :], cont_skip[:, 1:NG + 1], start=False, stop=True)
            mm.then_inc(nodes_mm, 1)
            pe.wait_ge(windows_ready, 1)
            pe.transpose(p_rows[:, 0, :], w_in[:, 0, :], ident[:, :])
            pe.transpose(p_rows[:, 1, :], w_in[:, 1, :], ident[:, :]).then_inc(w_turned, 1)

            def turn(g):
                pe.wait_ge(codes_ready, 3 * (g + 1))
                if not (isinstance(g, int) and g <= 1):
                    pe.wait_ge(deg_max_done, g - 1)
                for c in range(3):
                    mm = pe.transpose(p_tabs[:, c, :], codes[:, c, :], ident16[:, :])
                mm.then_inc(tabs_mm, 1)

            pe.wait_ge(nodes_ready, 1)
            turn(0)

            pe.wait_ge(w_ready, 2)
            pe.wait_ge(bc_out, BCS)
            def turn_h(n):
                t, k = self_batches[n]
                pe.wait_ge(lo_ready, (t + k - 1) // BT + 1)
                if n >= 2:
                    pe.wait_ge(ht_ready, n - 1)
                for j in range(k):
                    mm = pe.transpose(p_main[:, n % 2, j * 128:j * 128 + NP], h_f32[:, t + j, :], ident[0:NP, 0:NP])
                mm.then_inc(h_turned, 1)

            turn_h(0)
            for n, (t, k) in enumerate(self_batches):
                if n + 1 < len(self_batches):
                    turn_h(n + 1)
                pe.wait_ge(ht_ready, n + 1)
                if n >= 2:
                    pe.wait_ge(self_ready, n - 1)
                for j in range(k):
                    o = p_cnt[0:NP, 1, n % 2, j * D:(j + 1) * D]
                    pe.matmul(o, h_t[:, n % 2, j, :], ws_t[:, :], start=True, stop=False)
                    mm = pe.matmul(o, ones[0:1, 0:NP], b_row[:, :], start=False, stop=True)
                mm.then_inc(self_mm, 1)

            pe.wait_ge(self_ready, len(self_batches))

            def counts(g, par, u):
                pe.wait_ge(onehots_ready, UPG * g + u + 1)
                if not (isinstance(g, int) and g == 0 and u < 2):
                    pe.wait_ge(slab_written, UPG * g + u - 1)
                for s in range(US):
                    o = p_cnt[:, u % 2, s // 2, 0:2 * MC].rearrange("p (t s r) -> p t s r", s=2, r=WIN)[:, :, s % 2, :]
                    mm = pe.matmul(o, oh_part[:, u % RING, s, :], oh_cell[:, u % RING, s, :].rearrange("p (t r) -> p t r", r=WIN),
                                   start=(s % 2 == 0), stop=(s % 2 == 1), skip_group_check=True)
                mm.then_inc(counts_mm, 1)

            def products(g, par, a0, a1):
                for m in range(a0, a1):
                    a, part = m // 2, m % 2
                    mm = pe.matmul(p_main[:, par, 0:NCOL], (h_hi, h_lo)[part][:, a, :], slab[0:NP, par, a, :],
                                   start=(m == 0), stop=(m == 2 * NT - 1))
                return mm

            def group(g, par, build=True, prod=True, free=True, has_rows=True, codes_next=True, wait_rows=True):
                nb = UPG - FREE_UNITS
                for u in range(UPG):
                    if build:
                        counts(g, par, u)
                    if prod and u >= FREE_UNITS:
                        if u == FREE_UNITS:
                            pe.wait_ge(slab_written, UPG * g)
                            if free:
                                pe.wait_ge(sums_ready, g - 2)
                        j = u - FREE_UNITS
                        mm = products(None, 1 - par, 2 * NT * j // nb, 2 * NT * (j + 1) // nb)
                        if u == UPG - 1:
                            mm.then_inc(main_mm, 1)
                    if u == 4 and codes_next:
                        turn(g + 1)
                    if u == 8 and build:
                        pe.wait_ge(slot_ready, g + 1)
                        pe.wait_ge(tabs_ready, g + 2 if codes_next else g + 1)
                        if not (isinstance(g, int) and g == 0):
                            pe.wait_ge(deg_scanned, g)
                        for r in range(WIN):
                            mm = pe.matmul(p_deg, slot_sel[:, r, :], slot_oh[:, r, :], start=(r == 0), stop=(r == WIN - 1))
                        mm.then_inc(deg_mm, 1)
                    if u == 16 and build:
                        pe.wait_ge(diag_ready, g + 1)
                        for q in range(Q):
                            mm = pe.matmul(p_degr[:, q:q + 1], deg_diag[:, q * KQ:(q + 1) * KQ, :].rearrange("p k r -> p (k r)"),
                                           ones[0:WIN, 0:1], start=True, stop=True)
                        mm.then_inc(degr_mm, 1)
                    if u == 10 and has_rows:
                        pe.wait_ge(sums_ready, g - 1)
                        if wait_rows:
                            pe.wait_ge(rows_ready, g - 2)
                        for q in range(Q):
                            mm = pe.matmul(p_rows[0:RQ, q, :], sums[:, par, q * RQ:(q + 1) * RQ], wm_t[:, :], start=True, stop=True)
                        mm.then_inc(rows_mm, 1)

            pe.wait_ge(lo_ready, NB)
            group(0, 0, prod=False, has_rows=False)
            group(1, 1, free=False, has_rows=False)
            group(2, 0, free=False, wait_rows=False)
            group(3, 1)
            with pe.Fori(2, NG // 2 - 1) as i:
                group(2 * i, 0)
                group(2 * i + 1, 1)
            group(NG - 2, 0)
            group(NG - 1, 1, codes_next=False)
            group(NG, 0, build=False, codes_next=False)
            group(NG + 1, 1, build=False, prod=False, codes_next=False)


_INS = ["x", "src", "dst", "L0_gnn_W_msg", "L0_gnn_W_self", "L0_gnn_b_self", "L0_gnn_gamma", "L0_gnn_beta"]


def kernel(**inputs):
    import concourse.bacc as bacc
    from concourse.bass_utils import run_bass_kernel_spmd

    nc = bacc.Bacc("TRN2", target_bir_lowering=False, num_devices=1)
    arrays, args = {}, []
    for name in _INS:
        a = np.ascontiguousarray(inputs[name])
        arrays[f"in_{name}"] = a
        args.append(nc.dram_tensor(f"in_{name}", a.shape, mybir.dt.from_np(a.dtype), kind="ExternalInput").ap())
    out = nc.dram_tensor("out", inputs["x"].shape, F32, kind="ExternalOutput").ap()
    build_layer(nc, *args, out)
    r = run_bass_kernel_spmd(nc, [arrays], core_ids=[0])
    return r.results[0]["out"]
```

```python
import numpy as np
import concourse.bass as bass
import concourse.mybir as mybir
from concourse.alu_op_type import AluOpType as ALU

ACT = mybir.ActivationFunctionType
F32 = mybir.dt.float32
F16 = mybir.dt.float16
I32 = mybir.dt.int32
U32 = mybir.dt.uint32

EPS = 1e-5
MAGIC = float(3 << 22)
HSCALE = 4096.0
SKIP = float(1 << 18)


def build_layer(nc, x, src, dst, w_msg, w_self, b_self, gamma, beta, out):
    N, D = x.shape
    E = src.shape[0]
    NP = 125
    NT = N // NP
    EC = 125
    NCH = E // EC
    WIN = 2
    NWIN = -(-N // WIN)
    G = 120
    NG = -(-(NCH + NWIN - 1) // G)
    NCOL = G * WIN
    PCOL = 256
    MC = NT * WIN
    US = 5
    UPG = G // US
    UPB = 3
    BS = UPB * US
    BPG = UPG // UPB
    RING = 4
    CB = 3
    CP = 100
    CI = NCH // CP
    BT = 10
    NB = NT // BT
    FREE_UNITS = 2
    assert NP * NT == N and EC * NCH == E and CP * CI == NCH and NG % 2 == 0 and BT * NB == NT
    assert MC * US <= 512 and UPG % UPB == 0 and BPG % RING == 0 and NCOL <= PCOL and UPG % CB == 0

    agg_rows = nc.dram_tensor("agg_rows", [N, D], F32, kind="Internal").ap()

    def sb(name, shape, dt):
        return nc.alloc_sbuf_tensor(name, shape, dt)

    def ps(name, shape, dt=F32):
        return nc.alloc_psum_tensor(name, shape, dt)

    def sem(name):
        return nc.alloc_semaphore(name)

    h_f32 = sb("h_f32", [NP, NT, D], F32)
    h_hi = sb("h_hi", [NP, NT, D], F16)
    h_lo = sb("h_lo", [NP, NT, D], F16)
    slab = sb("slab", [128, 2, NT, PCOL], F16)
    work = slab[:].rearrange("p b t c -> p (b t c)").bitcast(F32)
    x_in = work[0:NP, 0:NT * D].rearrange("p (t d) -> p t d", d=D)
    x_res = work[0:NP, 0:NT * D].rearrange("p (t d) -> p t d", d=D)
    agg_in = work[0:NP, NT * D:2 * NT * D].rearrange("p (t d) -> p t d", d=D)
    oh_part = sb("oh_part", [EC, RING, BS, 128], F16)
    oh_cell = sb("oh_cell", [EC, RING, BS, MC], F16)
    same_win = sb("same_win", [128, NG * G], F32)
    steps_bc = sb("steps_bc", [G, NG, G], F16)
    code_f = sb("code_f", [G, 8, EC], F32)
    codes = sb("codes", [G, 3, EC], F16)
    tabs = sb("tabs", [EC, 2, 3, G, 2], F16)
    dst_rows = sb("dst_rows", [G, 2, EC], I32)
    src_rows = sb("src_rows", [G, 2, EC], I32)
    chunk_of = sb("chunk_of", [G, NG], U32)
    chunk_col = sb("chunk_col", [G, 2, 1], U32)
    slot_base = sb("slot_base", [G, NG], F32)
    slot_col = sb("slot_col", [G, 2, 1], F32)
    node_of = sb("node_of", [G, NG, WIN], U32)
    node_col = sb("node_col", [G, 2, WIN], U32)
    node_base = sb("node_base", [G, NG], F32)
    slot_oh = sb("slot_oh", [EC, WIN, G], F16)
    deg_scan = sb("deg_scan", [WIN, 2, G], F32)
    deg_max = sb("deg_max", [G, WIN], F32)
    deg_inv = sb("deg_inv", [G, NG, WIN], F32)
    sums = sb("sums", [D, 2, NCOL], F32)
    rows = sb("rows", [G, 2, WIN, D], F32)
    wm_t = sb("wm_t", [D, D], F32)
    ws_t = sb("ws_t", [D, D], F32)
    w_in = sb("w_in", [D, 2, D], F32)
    b_row = sb("b_row", [1, D], F32)
    gamma_bc = sb("gamma_bc", [NP, D], F32)
    beta_bc = sb("beta_bc", [NP, D], F32)
    zero_row = sb("zero_row", [NP, D], F32)
    stats = sb("stats", [NP, BT, 6], F32)
    mv = sb("mv", [NP, NT, 2], F32)
    rstd = sb("rstd", [NP, NT, 2], F32)
    h_t = sb("h_t", [D, 2, 4, NP], F32)
    diff = sb("diff", [128, 128], F32)
    ident = sb("ident", [128, 128], F32)
    ident16 = sb("ident16", [G, G], F16)
    tri_lt = sb("tri_lt", [CP, CP], F32)
    tri_le = sb("tri_le", [G, G], F32)
    ones = sb("ones", [128, 128], F32)
    ones16 = sb("ones16", [G, 128], F16)
    iota_part = sb("iota_part", [EC, 128], F16)
    iota_cell = sb("iota_cell", [EC, MC], F16)
    iota_g = sb("iota_g", [CP, G], F32)
    iota_slot = sb("iota_slot", [EC, WIN], F32)
    step_no = sb("step_no", [G, NG], F32)
    next_step = sb("next_step", [G, G], F32)
    next_group = sb("next_group", [G, G], F32)
    slot_sel = sb("slot_sel", [EC, WIN, WIN], F16)
    slot_src = sb("slot_src", [EC, WIN, WIN], F32)
    ends = sb("ends", [CP, 3, CI], I32)
    ends_f = sb("ends_f", [CP, 3, CI], F32)
    wins = sb("wins", [CP, 3, CI], F32)
    n_steps = sb("n_steps", [CP, CI], F32)
    steps_inc = sb("steps_inc", [CP, CI], F32)
    steps_before = sb("steps_before", [CP, 1], F32)
    start = sb("start", [CP, CI], F32)
    start_gf = sb("start_gf", [CP, CI], F32)
    start_g = sb("start_g", [CP, CI], F32)
    start_k = sb("start_k", [CP, CI], F32)
    jump = sb("jump", [CP, CI], F32)
    oh_k = sb("oh_k", [CP, CI, G], F32)
    oh_g = sb("oh_g", [CP, CI, 2, NG], F32)
    marks = sb("marks", [G, 2, NG], F32)
    tot_scan = sb("tot_scan", [G, 2, NG], F32)
    tot_ex = sb("tot_ex", [G, 2, NG], F32)
    prefix = sb("prefix", [G, 2, NG], F32)
    window = sb("window", [G, NG], F32)
    cont = sb("cont", [G, NG], F32)
    cont_skip = sb("cont_skip", [G, NG + 1], F32)

    p_cnt = ps("p_cnt", [128, CB, 512])
    p_main = ps("p_main", [128, 2, 512])
    p_misc = ps("p_misc", [128, 512])
    p_degs = ps("p_degs", [128, 512])
    p_rows = ps("p_rows", [128, 4, D])
    p_tabs = p_misc[0:EC, 0:192].bitcast(F16).rearrange("p (c k) -> p c k", c=3)[:, :, 0:G]
    p_deg = p_degs[0:WIN, 0:G]
    p_degr = p_degs[0:G, 384:384 + WIN]

    x_landed = [sem(f"x_landed{b}") for b in range(NB)]
    w_landed = sem("w_landed")
    ends_landed = sem("ends_landed")
    zeroed = sem("zeroed")
    zero_ready = sem("zero_ready")
    ends_set = sem("ends_set")
    iotas = sem("iotas")
    dve = sem("dve")
    consts_ready = sem("consts_ready")
    mv_ready = sem("mv_ready")
    std_ready = sem("std_ready")
    y_ready = sem("y_ready")
    relu_ready = sem("relu_ready")
    hi_ready = sem("hi_ready")
    lo_ready = sem("lo_ready")
    w_turned = sem("w_turned")
    w_ready = sem("w_ready")
    h_turned = sem("h_turned")
    ht_ready = sem("ht_ready")
    self_mm = sem("self_mm")
    self_ready = sem("self_ready")
    inc_ready = sem("inc_ready")
    before_mm = sem("before_mm")
    oh_steps = sem("oh_steps")
    marks_mm = sem("marks_mm")
    marks_ready = sem("marks_ready")
    prefix_mm = sem("prefix_mm")
    chunks_ready = sem("chunks_ready")
    windows_ready = sem("windows_ready")
    nodes_mm = sem("nodes_mm")
    nodes_ready = sem("nodes_ready")
    bc_ready = sem("bc_ready")
    bc_mm = sem("bc_mm")
    bc_out = sem("bc_out")
    gathered = [sem("gathered0"), sem("gathered1")]
    col_copied = sem("col_copied")
    pool_waits = sem("pool_waits")
    pool = sem("pool")
    codes_ready = sem("codes_ready")
    tabs_mm = sem("tabs_mm")
    tabs_ready = sem("tabs_ready")
    onehots_ready = sem("onehots_ready")
    counts_mm = sem("counts_mm")
    slab_written = sem("slab_written")
    main_mm = sem("main_mm")
    sums_ready = sem("sums_ready")
    slot_ready = sem("slot_ready")
    deg_mm = sem("deg_mm")
    deg_scanned = sem("deg_scanned")
    degr_mm = sem("degr_mm")
    deg_max_done = sem("deg_max_done")
    deg_ready = sem("deg_ready")
    rows_mm = sem("rows_mm")
    rows_ready = sem("rows_ready")
    node_copied = sem("node_copied")
    scattered = [sem("scattered0"), sem("scattered1")]
    x_back = sem("x_back")
    agg_landed = [sem(f"agg_landed{b}") for b in range(NB)]
    xb_ready = sem("xb_ready")
    o_ready = sem("o_ready")
    o_relu = sem("o_relu")
    mv2_ready = sem("mv2_ready")
    std2_ready = sem("std2_ready")
    n_ready = sem("n_ready")
    gam_ready = sem("gam_ready")
    out_ready = sem("out_ready")
    stored = sem("stored")

    x_nodes = x.rearrange("(p t) d -> p t d", t=NT)
    out_nodes = out.rearrange("(p t) d -> p t d", t=NT)
    agg_nodes = agg_rows.rearrange("(p t) d -> p t d", t=NT)
    dst_chunks = dst.rearrange("(c e) -> c e", e=EC)
    src_chunks = src.rearrange("(c e) -> c e", e=EC)
    dst_ends = dst.rearrange("(p i e) -> p i e", i=CI, e=EC)

    self_batches = [(t, min(4, NT - t)) for t in range(0, NT, 4)]
    NBC = 400
    BCS = NG * G // NBC

    with nc.Block() as block:

        @block.sync
        def _(sp):
            with nc.allow_non_contiguous_dma(reason="one destination per chunk end"):
                sp.dma_start(ends[:, 0, :], dst_ends[:, :, 0]).then_inc(ends_landed, 16)
                sp.dma_start(ends[:, 1, :], dst_ends[:, :, EC - 1]).then_inc(ends_landed, 16)
                sp.dma_start(ends[:, 2, 1:CI], dst_ends[:, 0:CI - 1, EC - 1]).then_inc(ends_landed, 16)
                sp.dma_start(ends[1:CP, 2, 0:1], dst_ends[0:CP - 1, CI - 1:CI, EC - 1]).then_inc(ends_landed, 16)
            for b in range(NB):
                sp.dma_start(x_in[:, b * BT:(b + 1) * BT, :], x_nodes[:, b * BT:(b + 1) * BT, :]).then_inc(x_landed[b], 16)
            sp.dma_start(w_in[:, 0, :], w_msg).then_inc(w_landed, 16)
            sp.dma_start(w_in[:, 1, :], w_self).then_inc(w_landed, 16)
            sp.dma_start(b_row[:, :], b_self.rearrange("(a d) -> a d", a=1)).then_inc(w_landed, 16)
            sp.dma_start(gamma_bc[:, :], gamma.rearrange("(a d) -> a d", a=1).to_broadcast([NP, D])).then_inc(w_landed, 16)
            sp.dma_start(beta_bc[:, :], beta.rearrange("(a d) -> a d", a=1).to_broadcast([NP, D])).then_inc(w_landed, 16)
            sp.wait_ge(zero_ready, 1)
            sp.dma_start(agg_nodes, zero_row[:, :].unsqueeze(1).to_broadcast([NP, NT, D])).then_inc(zeroed, 16)
            sp.wait_ge(main_mm, NG)
            sp.dma_start(x_res, x_nodes).then_inc(x_back, 16)
            sp.wait_ge(scattered[0], 16 * WIN * NG // 2)
            sp.wait_ge(scattered[1], 16 * WIN * NG // 2)
            for b in range(NB):
                t = slice(b * BT, (b + 1) * BT)
                sp.dma_start(agg_in[:, t, :], agg_nodes[:, t, :]).then_inc(agg_landed[b], 16)
            for b in range(NB):
                t = slice(b * BT, (b + 1) * BT)
                sp.wait_ge(out_ready, b + 1)
                sp.dma_start(out_nodes[:, t, :], agg_in[:, t, :]).then_inc(stored, 16)
            sp.wait_ge(stored, 16 * NB)

        @block.gpsimd
        def _(gp):
            nc.gpsimd.memset(ends[0:1, 2, 0:1], -WIN).then_inc(ends_set, 1)
            nc.gpsimd.memset(zero_row[:, :], 0.0).then_inc(zero_ready, 1)
            nc.gpsimd.iota(diff[:, :], [[-1, 128]], base=0, channel_multiplier=1, allow_small_or_imprecise_dtypes=True).then_inc(iotas, 1)
            nc.gpsimd.iota(iota_g[:, :], [[1, G]], base=0, channel_multiplier=0, allow_small_or_imprecise_dtypes=True).then_inc(iotas, 1)
            nc.gpsimd.iota(step_no[:, :], [[G, NG]], base=0, channel_multiplier=1, allow_small_or_imprecise_dtypes=True).then_inc(iotas, 1)
            nc.gpsimd.iota(slot_src[:, :, :], [[1, WIN], [-1, WIN]], base=0, channel_multiplier=0, allow_small_or_imprecise_dtypes=True).then_inc(iotas, 1)
            nc.gpsimd.iota(iota_part[:, :], [[1, 128]], base=0, channel_multiplier=0, allow_small_or_imprecise_dtypes=True).then_inc(iotas, 1)
            nc.gpsimd.iota(iota_cell[:, :], [[1, MC]], base=1, channel_multiplier=0, allow_small_or_imprecise_dtypes=True).then_inc(iotas, 1)
            nc.gpsimd.iota(iota_slot[:, :], [[1, WIN]], base=1, channel_multiplier=0, allow_small_or_imprecise_dtypes=True).then_inc(iotas, 1)

            def await_count(sem, value):
                gp.wait_ge(sem, value)
                gp.sem_inc(pool_waits, 1)

            def gather(g, par, i):
                await_count(col_copied, i)
                for rows_t, chunks in ((dst_rows, dst_chunks), (src_rows, src_chunks)):
                    gp.indirect_dma_start(out=rows_t[:, par, :], out_offset=None, in_=chunks,
                                          in_offset=bass.IndirectOffsetOnAxis(ap=chunk_col[:, par, :], axis=0),
                                          bounds_check=NCH - 1, oob_is_err=False).then_inc(gathered[par], 16)

            def copy_cols(par, col):
                gp.tensor_copy(chunk_col[:, par, :], chunk_of[:, col]).then_inc(col_copied, 1)

            NOPS = 11

            def make_codes(par, col, n_gathered, p0, n_turned):
                slot, off, far, part_f, part, four, rest, cell = (code_f[:, j, :] for j in range(8))
                gp.tensor_copy(slot_col[:, par, :], slot_base[:, col]).then_inc(pool, 1)
                await_count(gathered[par], n_gathered)
                await_count(pool, p0 + 1)
                gp.tensor_scalar(slot, dst_rows[:, par, :], slot_col[:, par, :], None, ALU.subtract).then_inc(pool, 1)
                gp.tensor_scalar(part_f, src_rows[:, par, :], (NT - 1) / 2.0, 1.0 / NT, ALU.subtract, ALU.mult).then_inc(pool, 1)
                gp.tensor_scalar(four, src_rows[:, par, :], float(WIN), None, ALU.mult).then_inc(pool, 1)
                await_count(pool, p0 + 4)
                gp.tensor_scalar(off, slot, -(WIN + 1) / 2.0, None, ALU.add).then_inc(pool, 1)
                gp.tensor_scalar(part, part_f, MAGIC, MAGIC, ALU.add, ALU.subtract).then_inc(pool, 1)
                gp.tensor_tensor(four, four, slot, ALU.add).then_inc(pool, 1)
                await_count(pool, p0 + 7)
                gp.tensor_tensor(off, off, off, ALU.mult).then_inc(pool, 1)
                gp.tensor_scalar(rest, part, -float(NT * WIN), None, ALU.mult).then_inc(pool, 1)
                await_count(pool, p0 + 9)
                gp.tensor_scalar(far, off, WIN * WIN / 4.0, 16384.0, ALU.is_gt, ALU.mult).then_inc(pool, 1)
                await_count(pool, p0 + 10)
                gp.tensor_tensor(cell, four, far, ALU.add).then_inc(pool, 1)
                if n_turned is not None:
                    await_count(tabs_mm, n_turned)
                gp.tensor_copy(codes[:, 0, :], part).then_inc(codes_ready, 1)
                gp.tensor_copy(codes[:, 2, :], slot).then_inc(codes_ready, 1)
                await_count(pool, p0 + 11)
                gp.tensor_tensor(codes[:, 1, :], cell, rest, ALU.add).then_inc(codes_ready, 1)

            def scatter(par, col, n_rows, n_copied):
                if n_copied is not None:
                    await_count(scattered[par], n_copied)
                gp.tensor_copy(node_col[:, par, :], node_of[:, col, :]).then_inc(node_copied, 1)
                await_count(node_copied, n_rows)
                await_count(rows_ready, n_rows)
                for q in range(WIN):
                    gp.indirect_dma_start(out=agg_rows, out_offset=bass.IndirectOffsetOnAxis(ap=node_col[:, par, q:q + 1], axis=0),
                                          in_=rows[:, par, q, :], in_offset=None,
                                          bounds_check=N - 1, oob_is_err=False).then_inc(scattered[par], 16)

            def group(g, i, par, fetch=True, code=True, store=True, first_store=False):
                if fetch:
                    await_count(codes_ready, 3 * (g + 1))
                    copy_cols(par, one(g + 2))
                    gather(None, par, g + 3)
                if code:
                    par1 = 1 - par
                    make_codes(par1, one(g + 1), 32 * (i + 1 + par), NOPS * (g + 1), g + 1)
                if store:
                    scatter(par, g - 2, g - 1, None if first_store else 16 * WIN * (i - 1))

            def one(a):
                return bass.ds(a, 1)

            gp.wait_ge(chunks_ready, 1)
            copy_cols(0, slice(0, 1))
            copy_cols(1, slice(1, 2))
            gather(None, 0, 1)
            gather(None, 1, 2)
            gp.wait_ge(windows_ready, 1)
            make_codes(0, slice(0, 1), 32, 0, None)
            gp.wait_ge(nodes_ready, 1)
            gp.wait_ge(zeroed, 16)
            gp.wait_ge(consts_ready, 1)
            group(0, 0, 0, store=False)
            group(1, 0, 1, store=False)
            group(2, 1, 0, first_store=True)
            group(3, 1, 1, first_store=True)
            with gp.Fori(2, NG // 2 - 1) as i:
                group(2 * i, i, 0)
                group(2 * i + 1, i, 1)
            group(NG - 2, NG // 2 - 1, 0, fetch=False)
            group(NG - 1, NG // 2 - 1, 1, fetch=False, code=False)
            group(NG, NG // 2, 0, fetch=False, code=False)
            group(NG + 1, NG // 2, 1, fetch=False, code=False)

            gp.wait_ge(x_back, 16)
            gp.wait_ge(w_landed, 80)
            gp.tensor_tensor(x_res, x_res, beta_bc[:, :].unsqueeze(1).to_broadcast([NP, NT, D]), ALU.add).then_inc(xb_ready, 1)
            gp.wait_ge(xb_ready, 1)
            for b in range(NB):
                t = slice(b * BT, (b + 1) * BT)
                gp.wait_ge(n_ready, b + 1)
                gp.tensor_tensor(agg_in[:, t, :], agg_in[:, t, :], gamma_bc[:, :].unsqueeze(1).to_broadcast([NP, BT, D]), ALU.mult).then_inc(gam_ready, 1)
                gp.wait_ge(gam_ready, b + 1)
                gp.tensor_tensor(agg_in[:, t, :], agg_in[:, t, :], x_res[:, t, :], ALU.add).then_inc(out_ready, 1)

        def turn_codes(act, g, par=0):
            act.wait_ge(tabs_mm, g + 1)
            if not isinstance(g, int) or g >= 2:
                act.wait_ge(onehots_ready, BPG * (g - 1))
                act.wait_ge(slot_ready, g - 1)
            act.activation(tabs[:, par, :, :, :], p_tabs.unsqueeze(3).to_broadcast([EC, 3, G, 2]), ACT.Copy).then_inc(tabs_ready, 1)

        @block.scalar
        def _(act):
            for j in range(BCS):
                act.wait_ge(bc_mm, j + 1)
                act.activation(same_win[:, j * NBC:(j + 1) * NBC], p_cnt[:, j % CB, 0:NBC], ACT.Copy).then_inc(bc_out, 1)
            act.wait_ge(w_turned, 1)
            act.activation(wm_t[:, :], p_rows[:, 0, :], ACT.Copy, scale=1.0 / HSCALE).then_inc(w_ready, 1)
            act.activation(ws_t[:, :], p_rows[:, 1, :], ACT.Copy).then_inc(w_ready, 1)
            for b in range(NB):
                t = slice(b * BT, (b + 1) * BT)
                act.wait_ge(mv_ready, b + 1)
                act.activation(rstd[:, t, 0], mv[:, t, 1], ACT.Sqrt).then_inc(std_ready, 1)
                act.wait_ge(y_ready, b + 1)
                act.activation(h_f32[:, t, :], h_f32[:, t, :], ACT.Relu).then_inc(relu_ready, 1)
                act.wait_ge(relu_ready, b + 1)
                act.activation(h_hi[:, t, :], h_f32[:, t, :], ACT.Copy, scale=HSCALE).then_inc(hi_ready, 1)
            turn_codes(act, 0)
            for n, (t, k) in enumerate(self_batches):
                act.wait_ge(h_turned, n + 1)
                if n >= 2:
                    act.wait_ge(self_mm, n - 1)
                act.activation(h_t[:, n % 2, 0:k, :], p_main[:, n % 2, :].rearrange("p (t e) -> p t e", t=4)[:, 0:k, 0:NP], ACT.Copy).then_inc(ht_ready, 1)

            def group(g, par, counts=True, codes_next=True, has_rows=True, guard_rows=True):
                for u in range(UPG):
                    if counts:
                        act.wait_ge(counts_mm, UPG * g + u + 1)
                        if u == 0 and (not isinstance(g, int) or g >= 2):
                            act.wait_ge(main_mm, g - 1)
                        act.activation(slab[:, par, :, u * US * WIN:(u + 1) * US * WIN],
                                       p_cnt[:, u % CB, 0:US * MC].rearrange("p (t c) -> p t c", t=NT), ACT.Copy).then_inc(slab_written, 1)
                    if u == 13 and codes_next:
                        turn_codes(act, g + 1, 1 - par)
                    if u == 16 and has_rows:
                        act.wait_ge(rows_mm, g - 1)
                        act.wait_ge(deg_ready, g - 1)
                        if guard_rows:
                            act.wait_ge(scattered[par], 8 * WIN * (g - par) - 16 * WIN)
                        for q in range(WIN):
                            last = act.activation(rows[:, par, q, :], p_rows[0:G, q, :], ACT.Copy, scale=deg_inv[:, g - 2, q:q + 1])
                        last.then_inc(rows_ready, 1)

            group(0, 0, has_rows=False)
            group(1, 1, has_rows=False)
            group(2, 0, guard_rows=False)
            group(3, 1, guard_rows=False)
            with act.Fori(2, NG // 2 - 1) as i:
                group(2 * i, 0)
                group(2 * i + 1, 1)
            group(NG - 2, 0)
            group(NG - 1, 1, codes_next=False)
            group(NG, 0, counts=False, codes_next=False)
            group(NG + 1, 1, counts=False, codes_next=False)

            for b in range(NB):
                t = slice(b * BT, (b + 1) * BT)
                act.wait_ge(o_ready, b + 1)
                act.activation(agg_in[:, t, :], agg_in[:, t, :], ACT.Relu).then_inc(o_relu, 1)
                act.wait_ge(mv2_ready, b + 1)
                act.activation(rstd[:, t, 0], mv[:, t, 1], ACT.Sqrt).then_inc(std2_ready, 1)

        @block.vector
        def _(v):
            done = [0]

            def own(ins):
                done[0] += 1
                ins.then_inc(dve, 1)
                v.wait_ge(dve, done[0])

            v.wait_ge(iotas, 7)
            v.tensor_scalar(ident[:, :], diff[:, :], 0.0, None, ALU.is_equal)
            v.tensor_scalar(ident16[:, :], diff[0:G, 0:G], 0.0, None, ALU.is_equal)
            v.tensor_scalar(tri_lt[:, :], diff[0:CP, 0:CP], 0.0, None, ALU.is_lt)
            v.tensor_scalar(tri_le[:, :], diff[0:G, 0:G], 0.0, None, ALU.is_le)
            v.tensor_scalar(next_step[:, :], diff[0:G, 0:G], 1.0, None, ALU.is_equal)
            v.tensor_scalar(next_group[:, :], diff[0:G, 0:G], float(1 - G), None, ALU.is_equal)
            v.tensor_scalar(slot_sel[:, :, :], slot_src[:, :, :], 0.0, None, ALU.is_equal)
            v.memset(ones[:, :], 1.0)
            v.memset(ones16[:, :], 1.0)
            v.memset(cont_skip[:, :], 0.0).then_inc(consts_ready, 1)

            v.wait_ge(ends_landed, 64)
            v.wait_ge(ends_set, 1)
            own(v.tensor_scalar(ends_f[:, :, :], ends[:, :, :], (WIN - 1) / 2.0, 1.0 / WIN, ALU.subtract, ALU.mult))
            own(v.tensor_scalar(wins[:, :, :], ends_f[:, :, :], MAGIC, MAGIC, ALU.add, ALU.subtract))
            own(v.scalar_tensor_tensor(out=n_steps[:, :], in0=wins[:, 1, :], scalar=1.0, in1=wins[:, 0, :], op0=ALU.add, op1=ALU.subtract))
            v.tensor_tensor_scan(steps_inc[:, :], ones[0:CP, 0:CI], n_steps[:, :], 0.0, ALU.mult, ALU.add).then_inc(inc_ready, 1)
            v.scalar_tensor_tensor(out=jump[:, :], in0=wins[:, 0, :], scalar=-1.0, in1=wins[:, 2, :], op0=ALU.add, op1=ALU.subtract)
            v.wait_ge(before_mm, 1)
            own(v.tensor_copy(steps_before[:, :], p_misc[0:CP, 0:1]))
            own(v.scalar_tensor_tensor(out=start[:, :], in0=steps_inc[:, :], scalar=steps_before[:, :], in1=n_steps[:, :], op0=ALU.add, op1=ALU.subtract))
            own(v.tensor_scalar(start_gf[:, :], start[:, :], (G - 1) / 2.0, 1.0 / G, ALU.subtract, ALU.mult))
            own(v.tensor_scalar(start_g[:, :], start_gf[:, :], MAGIC, MAGIC, ALU.add, ALU.subtract))
            own(v.scalar_tensor_tensor(out=start_k[:, :], in0=start_g[:, :], scalar=-float(G), in1=start[:, :], op0=ALU.mult, op1=ALU.add))
            v.tensor_tensor(oh_k[:, :, :], iota_g[:, :].unsqueeze(1).to_broadcast([CP, CI, G]),
                            start_k[:, :].unsqueeze(2).to_broadcast([CP, CI, G]), ALU.is_equal)
            own(v.tensor_tensor(oh_g[:, :, 0, :], iota_g[:, 0:NG].unsqueeze(1).to_broadcast([CP, CI, NG]),
                                start_g[:, :].unsqueeze(2).to_broadcast([CP, CI, NG]), ALU.is_equal))
            v.tensor_tensor(oh_g[:, :, 1, :], oh_g[:, :, 0, :], jump[:, :].unsqueeze(2).to_broadcast([CP, CI, NG]), ALU.mult).then_inc(oh_steps, 1)
            v.wait_ge(marks_mm, 1)
            v.tensor_copy(marks[:, :, :], p_misc[0:G, 0:2 * NG].rearrange("p (h g) -> p h g", h=2)).then_inc(marks_ready, 1)
            v.wait_ge(marks_ready, 1)
            own(v.tensor_scalar(cont[:, :], marks[:, 1, :], -1.0, None, ALU.is_equal))
            v.tensor_tensor(steps_bc[:, :, :], ident16[:, :].unsqueeze(1).to_broadcast([G, NG, G]),
                            cont[:, :].unsqueeze(2).to_broadcast([G, NG, G]), ALU.mult).then_inc(bc_ready, 1)
            v.wait_ge(consts_ready, 1)
            v.tensor_scalar(cont_skip[:, 0:NG], cont[:, :], SKIP, None, ALU.mult)
            v.wait_ge(prefix_mm, 1)
            totals = p_rows[0:G, 0, 0:2 * NG].rearrange("p (h g) -> p h g", h=2)
            within = p_rows[0:G, 1, 0:2 * NG].rearrange("p (h g) -> p h g", h=2)
            v.tensor_tensor_scan(tot_scan[:, 0, :], ones[0:G, 0:NG], totals[:, 0, :], 0.0, ALU.mult, ALU.add)
            own(v.tensor_tensor_scan(tot_scan[:, 1, :], ones[0:G, 0:NG], totals[:, 1, :], 0.0, ALU.mult, ALU.add))
            own(v.tensor_tensor(tot_ex[:, :, :], tot_scan[:, :, :], totals, ALU.subtract))
            own(v.tensor_tensor(prefix[:, :, :], tot_ex[:, :, :], within, ALU.add))
            v.tensor_scalar(chunk_of[:, :], prefix[:, 0, :], -1.0, None, ALU.add).then_inc(chunks_ready, 1)
            own(v.tensor_tensor(window[:, :], prefix[:, 1, :], step_no[:, :], ALU.add))
            v.tensor_scalar(slot_base[:, :], window[:, :], float(WIN), -1.0, ALU.mult, ALU.add).then_inc(windows_ready, 1)
            v.wait_ge(nodes_mm, 1)
            own(v.scalar_tensor_tensor(out=node_base[:, :], in0=window[:, :], scalar=float(WIN), in1=p_misc[0:G, 0:NG], op0=ALU.mult, op1=ALU.add))
            for r in range(WIN):
                last = v.tensor_scalar(node_of[:, :, r], node_base[:, :], float(r), None, ALU.add)
            last.then_inc(nodes_ready, 1)

            def tile_stats(src_t, t0, n_ready):
                for j in range(BT):
                    last = v.bn_stats(stats[:, j, :], src_t[:, t0 + j, :])
                own(last)
                for j in range(BT):
                    last = v.bn_aggr(mv[:, t0 + j, :], stats[:, j, :])
                own(last)
                v.tensor_scalar(mv[:, t0:t0 + BT, 1], mv[:, t0:t0 + BT, 1], EPS, None, ALU.add).then_inc(n_ready, 1)

            for b in range(NB):
                t0 = b * BT
                t = slice(t0, t0 + BT)
                v.wait_ge(x_landed[b], 16)
                tile_stats(x_in, t0, mv_ready)
                v.wait_ge(std_ready, b + 1)
                own(v.reciprocal(rstd[:, t, 1], rstd[:, t, 0]))
                for j in range(t0, t0 + BT):
                    last = v.tensor_scalar(h_f32[:, j, :], x_in[:, j, :], mv[:, j, 0:1], rstd[:, j, 1:2], ALU.subtract, ALU.mult)
                last.then_inc(y_ready, 1)
                v.wait_ge(hi_ready, b + 1)
                v.scalar_tensor_tensor(out=h_lo[:, t, :], in0=h_f32[:, t, :], scalar=HSCALE, in1=h_hi[:, t, :],
                                       op0=ALU.mult, op1=ALU.subtract).then_inc(lo_ready, 1)
            for n, (t, k) in enumerate(self_batches):
                v.wait_ge(self_mm, n + 1)
                v.tensor_copy(h_f32[:, t:t + k, :], p_cnt[0:NP, n % 2, 0:k * D].rearrange("p (t d) -> p t d", d=D)).then_inc(self_ready, 1)

            def group(g, par, build=True, join=True, first_join=False):
                if build:
                    v.wait_ge(tabs_ready, g + 1)
                for u in range(UPG):
                    if build and u % UPB == 0:
                        n = u // UPB
                        r = n % RING
                        if not (isinstance(g, int) and g == 0 and n < RING):
                            v.wait_ge(counts_mm, UPG * g + u + UPB * (1 - RING))
                        k = slice(u * US, u * US + BS)
                        v.tensor_tensor(oh_part[:, r, :, :].rearrange("p s (c e) -> p s c e", e=2),
                                        iota_part[:, :].rearrange("p (c e) -> p c e", e=2).unsqueeze(1).to_broadcast([EC, BS, 64, 2]),
                                        tabs[:, par, 0, k, :].unsqueeze(2).to_broadcast([EC, BS, 64, 2]), ALU.is_equal)
                        v.tensor_tensor(oh_cell[:, r, :, :].rearrange("p s (c e) -> p s c e", e=2),
                                        iota_cell[:, :].rearrange("p (c e) -> p c e", e=2).unsqueeze(1).to_broadcast([EC, BS, MC // 2, 2]),
                                        tabs[:, par, 1, k, :].unsqueeze(2).to_broadcast([EC, BS, MC // 2, 2]), ALU.is_equal).then_inc(onehots_ready, 1)
                    if build:
                        if u == 0:
                            if not (isinstance(g, int) and g == 0):
                                v.wait_ge(deg_mm, g)
                            v.tensor_tensor(slot_oh[:, :, :], tabs[:, par, 2, :, 0].unsqueeze(1).to_broadcast([EC, WIN, G]),
                                            iota_slot[:, :].unsqueeze(2).to_broadcast([EC, WIN, G]), ALU.is_equal).then_inc(slot_ready, 1)
                        if u == 9:
                            v.wait_ge(deg_mm, g + 1)
                            first = isinstance(g, int) and g == 0
                            if not first:
                                v.wait_ge(deg_scanned, g)
                            if not (isinstance(g, int) and g <= 1):
                                v.wait_ge(degr_mm, g - 1)
                            v.tensor_tensor_scan(deg_scan[:, par, :], same_win[0:WIN, at(g)], p_deg,
                                                 0.0 if first else deg_scan[:, 1 - par, G - 1:G], ALU.mult, ALU.add).then_inc(deg_scanned, 1)
                    if u == 21 and build:
                        v.wait_ge(degr_mm, g + 1)
                        if not (isinstance(g, int) and g == 0):
                            v.wait_ge(deg_ready, g)
                        v.tensor_scalar(deg_max[:, :], p_degr, 1.0, None, ALU.max).then_inc(deg_max_done, 1)
                        v.wait_ge(deg_max_done, g + 1)
                        v.reciprocal(deg_inv[:, g, :], deg_max[:, :]).then_inc(deg_ready, 1)
                    if u == 12 and join:
                        v.wait_ge(main_mm, g - 1)
                        if not first_join:
                            v.wait_ge(sums_ready, g - 2)
                            if not (isinstance(g, int) and g == 3):
                                v.wait_ge(rows_mm, g - 3)
                        for r4 in range(WIN):
                            last = v.tensor_tensor_scan(sums[:, par, r4:NCOL:WIN], same_win[:, at(g - 2)], p_main[:, par, r4:NCOL:WIN],
                                                        0.0 if first_join else sums[:, 1 - par, NCOL - WIN + r4:NCOL - WIN + r4 + 1],
                                                        ALU.mult, ALU.add)
                        last.then_inc(sums_ready, 1)

            def at(g):
                return bass.ds(g * G, G)

            group(0, 0, join=False)
            group(1, 1, join=False)
            group(2, 0, first_join=True)
            group(3, 1)
            with v.Fori(2, NG // 2) as i:
                group(2 * i, 0)
                group(2 * i + 1, 1)
            group(NG, 0, build=False)
            group(NG + 1, 1, build=False)

            for b in range(NB):
                t0 = b * BT
                t = slice(t0, t0 + BT)
                v.wait_ge(agg_landed[b], 16)
                v.wait_ge(self_ready, len(self_batches))
                v.tensor_tensor(agg_in[:, t, :], agg_in[:, t, :], h_f32[:, t, :], ALU.add).then_inc(o_ready, 1)
                v.wait_ge(o_relu, b + 1)
                tile_stats(agg_in, t0, mv2_ready)
                v.wait_ge(std2_ready, b + 1)
                own(v.reciprocal(rstd[:, t, 1], rstd[:, t, 0]))
                for j in range(t0, t0 + BT):
                    last = v.tensor_scalar(agg_in[:, j, :], agg_in[:, j, :], mv[:, j, 0:1], rstd[:, j, 1:2], ALU.subtract, ALU.mult)
                last.then_inc(n_ready, 1)

        @block.tensor
        def _(pe):
            pe.wait_ge(consts_ready, 1)
            pe.wait_ge(inc_ready, 1)
            pe.matmul(p_misc[0:CP, 0:1], tri_lt[:, :], steps_inc[:, CI - 1:CI], start=True, stop=True).then_inc(before_mm, 1)
            pe.wait_ge(w_landed, 80)
            pe.wait_ge(oh_steps, 1)
            for i in range(CI):
                mm = pe.matmul(p_misc[0:G, 0:2 * NG], oh_k[:, i, :], oh_g[:, i, :, :].rearrange("p h g -> p (h g)"),
                               start=(i == 0), stop=(i == CI - 1))
            mm.then_inc(marks_mm, 1)
            pe.wait_ge(marks_ready, 1)
            flat = marks[:, :, :].rearrange("p h g -> p (h g)")
            pe.matmul(p_rows[0:G, 0, 0:2 * NG], ones[0:G, 0:G], flat, start=True, stop=True)
            pe.matmul(p_rows[0:G, 1, 0:2 * NG], tri_le[:, :], flat, start=True, stop=True).then_inc(prefix_mm, 1)
            pe.wait_ge(bc_ready, 1)
            flat = steps_bc[:, :, :].rearrange("p g k -> p (g k)")
            for j in range(BCS):
                if j >= CB:
                    pe.wait_ge(bc_out, j - CB + 1)
                pe.matmul(p_cnt[:, j % CB, 0:NBC], ones16[:, :], flat[:, j * NBC:(j + 1) * NBC], start=True, stop=True).then_inc(bc_mm, 1)
            pe.wait_ge(windows_ready, 1)
            pe.matmul(p_misc[0:G, 0:NG], next_step[:, :], cont_skip[:, 0:NG], start=True, stop=False)
            pe.matmul(p_misc[0:G, 0:NG], next_group[:, :], cont_skip[:, 1:NG + 1], start=False, stop=True).then_inc(nodes_mm, 1)
            pe.wait_ge(windows_ready, 1)
            pe.transpose(p_rows[:, 0, :], w_in[:, 0, :], ident[:, :])
            pe.transpose(p_rows[:, 1, :], w_in[:, 1, :], ident[:, :]).then_inc(w_turned, 1)

            def turn(g):
                pe.wait_ge(codes_ready, 3 * (g + 1))
                if not (isinstance(g, int) and g == 0):
                    pe.wait_ge(tabs_ready, g)
                for c in range(3):
                    mm = pe.transpose(p_tabs[:, c, :], codes[:, c, :], ident16[:, :])
                mm.then_inc(tabs_mm, 1)

            pe.wait_ge(nodes_ready, 1)
            turn(0)

            pe.wait_ge(w_ready, 2)
            pe.wait_ge(bc_out, BCS)
            def turn_h(n):
                t, k = self_batches[n]
                pe.wait_ge(lo_ready, (t + k - 1) // BT + 1)
                if n >= 2:
                    pe.wait_ge(ht_ready, n - 1)
                for j in range(k):
                    mm = pe.transpose(p_main[:, n % 2, j * 128:j * 128 + NP], h_f32[:, t + j, :], ident[0:NP, 0:NP])
                mm.then_inc(h_turned, 1)

            turn_h(0)
            for n, (t, k) in enumerate(self_batches):
                if n + 1 < len(self_batches):
                    turn_h(n + 1)
                pe.wait_ge(ht_ready, n + 1)
                if n >= 2:
                    pe.wait_ge(self_ready, n - 1)
                for j in range(k):
                    o = p_cnt[0:NP, n % 2, j * D:(j + 1) * D]
                    pe.matmul(o, h_t[:, n % 2, j, :], ws_t[:, :], start=True, stop=False)
                    mm = pe.matmul(o, ones[0:1, 0:NP], b_row[:, :], start=False, stop=True)
                mm.then_inc(self_mm, 1)

            pe.wait_ge(self_ready, len(self_batches))

            def counts(g, par, u):
                if u % UPB == 0:
                    pe.wait_ge(onehots_ready, BPG * g + u // UPB + 1)
                if not (isinstance(g, int) and g == 0 and u < CB):
                    pe.wait_ge(slab_written, UPG * g + u + 1 - CB)
                for s in range(US):
                    k = u % UPB * US + s
                    o = p_cnt[:, u % CB, 0:US * MC].rearrange("p (t s r) -> p t s r", s=US, r=WIN)[:, :, s, :]
                    mm = pe.matmul(o, oh_part[:, u // UPB % RING, k, :], oh_cell[:, u // UPB % RING, k, :].rearrange("p (t r) -> p t r", r=WIN),
                                   start=(s == 0), stop=(s == US - 1), skip_group_check=True)
                mm.then_inc(counts_mm, 1)

            def products(g, par, a0, a1):
                for m in range(a0, a1):
                    a, part = m // 2, m % 2
                    mm = pe.matmul(p_main[:, par, 0:NCOL], (h_hi, h_lo)[part][:, a, :], slab[0:NP, par, a, 0:NCOL],
                                   start=(m == 0), stop=(m == 2 * NT - 1))
                return mm

            def group(g, par, build=True, prod=True, free=True, has_rows=True, codes_next=True, wait_rows=True):
                nb = UPG - FREE_UNITS
                for u in range(UPG):
                    if build:
                        counts(g, par, u)
                    if prod and u >= FREE_UNITS:
                        if u == FREE_UNITS:
                            pe.wait_ge(slab_written, UPG * g)
                            if free:
                                pe.wait_ge(sums_ready, g - 2)
                        j = u - FREE_UNITS
                        mm = products(None, 1 - par, 2 * NT * j // nb, 2 * NT * (j + 1) // nb)
                        if u == UPG - 1:
                            mm.then_inc(main_mm, 1)
                    if u == 12 and codes_next:
                        turn(g + 1)
                    if u == 1 and build:
                        pe.wait_ge(slot_ready, g + 1)
                        if not (isinstance(g, int) and g == 0):
                            pe.wait_ge(deg_max_done, g)
                        for r in range(WIN):
                            mm = pe.matmul(p_deg, slot_sel[:, r, :], slot_oh[:, r, :], start=(r == 0), stop=(r == WIN - 1))
                        mm.then_inc(deg_mm, 1)
                    if u == 12 and build:
                        pe.wait_ge(deg_scanned, g + 1)
                        mm = pe.matmul(p_degr, deg_scan[:, par, :], ident[0:WIN, 0:WIN], start=True, stop=True)
                        mm.then_inc(degr_mm, 1)
                    if u == 15 and has_rows:
                        pe.wait_ge(sums_ready, g - 1)
                        if wait_rows:
                            pe.wait_ge(rows_ready, g - 2)
                        for q in range(WIN):
                            mm = pe.matmul(p_rows[0:G, q, :], sums[:, par, q:NCOL:WIN], wm_t[:, :], start=True, stop=True)
                        mm.then_inc(rows_mm, 1)

            pe.wait_ge(lo_ready, NB)
            group(0, 0, prod=False, has_rows=False)
            group(1, 1, free=False, has_rows=False)
            group(2, 0, free=False, wait_rows=False)
            group(3, 1)
            with pe.Fori(2, NG // 2 - 1) as i:
                group(2 * i, 0)
                group(2 * i + 1, 1)
            group(NG - 2, 0)
            group(NG - 1, 1, codes_next=False)
            group(NG, 0, build=False, codes_next=False)
            group(NG + 1, 1, build=False, prod=False, codes_next=False)


_INS = ["x", "src", "dst", "L0_gnn_W_msg", "L0_gnn_W_self", "L0_gnn_b_self", "L0_gnn_gamma", "L0_gnn_beta"]


def kernel(**inputs):
    import concourse.bacc as bacc
    from concourse.bass_utils import run_bass_kernel_spmd

    nc = bacc.Bacc("TRN2", target_bir_lowering=False, num_devices=1)
    arrays, args = {}, []
    for name in _INS:
        a = np.ascontiguousarray(inputs[name])
        arrays[f"in_{name}"] = a
        args.append(nc.dram_tensor(f"in_{name}", a.shape, mybir.dt.from_np(a.dtype), kind="ExternalInput").ap())
    out = nc.dram_tensor("out", inputs["x"].shape, F32, kind="ExternalOutput").ap()
    build_layer(nc, *args, out)
    r = run_bass_kernel_spmd(nc, [arrays], core_ids=[0])
    return r.results[0]["out"]
```

```python
import numpy as np
import concourse.bass as bass
import concourse.mybir as mybir
from concourse.alu_op_type import AluOpType as ALU

ACT = mybir.ActivationFunctionType
F32 = mybir.dt.float32
F16 = mybir.dt.float16
I32 = mybir.dt.int32
U32 = mybir.dt.uint32

EPS = 1e-5
MAGIC = float(3 << 22)
HSCALE = 4096.0
SKIP = float(1 << 18)


def build_layer(nc, x, src, dst, w_msg, w_self, b_self, gamma, beta, out):
    N, D = x.shape
    E = src.shape[0]
    NP = 128
    NT = -(-N // NP)
    FP = N // NT
    RT = N - FP * NT
    EC = 125
    NCH = E // EC
    WIN = 2
    NWIN = -(-N // WIN)
    G = 120
    NG = -(-(NCH + NWIN - 1) // G)
    NCOL = G * WIN
    PCOL = 256
    MC = NT * WIN
    US = 5
    UPG = G // US
    UPB = 4
    BS = UPB * US
    BPG = UPG // UPB
    RING = 3
    CB = 3
    CP = 100
    CI = NCH // CP
    BT = 10
    NB = -(-NT // BT)
    KB = [min(BT, NT - b * BT) for b in range(NB)]
    FREE_UNITS = 2
    LU = -(-(NCH + NWIN - 1 - (NG - 1) * G) // US)
    LG = LU * US
    SLOT_STEP = 64
    CH = CI // 2
    ROW = 2 * EC
    assert FP == NP - 1 and RT > 0 and EC * NCH == E and CP * CI == NCH and NG % 2 == 0
    assert MC * US <= 512 and UPG % UPB == 0 and BPG % RING == 0 and NCOL <= PCOL and UPG % CB == 0 and 0 < LU < UPG and NT <= SLOT_STEP and CI % 2 == 0

    agg_rows = nc.dram_tensor("agg_rows", [N, D], F32, kind="Internal").ap()
    cont_rows = nc.dram_tensor("cont_rows", [NG, G], F32, kind="Internal").ap()
    chunk_rows = nc.dram_tensor("chunk_rows", [NCH, ROW], F32, kind="Internal").ap()

    def sb(name, shape, dt):
        return nc.alloc_sbuf_tensor(name, shape, dt)

    def ps(name, shape, dt=F32):
        return nc.alloc_psum_tensor(name, shape, dt)

    def sem(name):
        return nc.alloc_semaphore(name)

    last_blocks = [(t, BT) for t in range(0, NT - BT, BT)] + [((NB - 1) * BT, BT // 2), ((NB - 1) * BT + BT // 2, KB[-1] - BT // 2)]
    LB = len(last_blocks)
    FIRST_POOL_LN = 3
    POOL_ADDS = (2, 3, 4)
    DVE_OUT = (4, 5)

    x_f32 = sb("x_f32", [NP, NT, D], F32)
    h_f32 = sb("h_f32", [NP, NT, D], F32)
    h_hi = sb("h_hi", [NP, NT, D], F16)
    h_lo = sb("h_lo", [NP, NT, D], F16)
    slab = sb("slab", [128, 2, NT, PCOL], F16)
    agg_in = slab[0:NP].rearrange("p b t c -> p (b t c)").bitcast(F32)[:, 0:NT * D].rearrange("p (t d) -> p t d", d=D)
    oh_part = sb("oh_part", [EC, RING, BS, 128], F16)
    oh_cell = sb("oh_cell", [EC, RING, BS, MC], F16)
    same_win = sb("same_win", [128, NG * G], F32)

    def overlay(par, a, n):
        return slab[:, par].rearrange("p t c -> p (t c)")[:, a // 2:(a + n) // 2]

    OH_G = CI * 3 * NG * 2
    oh_g = overlay(0, 0, OH_G)[0:CP].rearrange("p (i h g) -> p i h g", i=CI, h=3)
    src_f = overlay(0, OH_G, CI * EC * 4)[0:CP].bitcast(F32).rearrange("p (i e) -> p i e", i=CI)
    src_in = overlay(0, OH_G, CI * EC * 4)[0:CP].bitcast(I32).rearrange("p (i e) -> p i e", i=CI)
    part_f = overlay(0, OH_G + CI * EC * 4, CI * EC * 4)[0:CP].bitcast(F32).rearrange("p (i e) -> p i e", i=CI)
    part_r = oh_part[0:CP].rearrange("p r s c -> p (r s c)").bitcast(F32)[:, 0:CI * EC].rearrange("p (i e) -> p i e", i=CI)
    packed = overlay(1, 0, CI * ROW * 4)[0:CP].bitcast(F32).rearrange("p (i w) -> p i w", i=CI)
    packed_h = overlay(1, 0, CI * ROW * 4)[0:CP].rearrange("p (i w) -> p i w", i=CI)[:, :, 2 * EC:4 * EC].rearrange("p i (c e) -> p i c e", c=2)
    oh_k = oh_cell[0:CP].rearrange("p r s c -> p (r s c)")[:, 0:CI * G].rearrange("p (i k) -> p i k", i=CI)
    dst_in = h_f32[0:CP].rearrange("p t d -> p (t d)").bitcast(I32)[:, 0:CI * EC].rearrange("p (i e) -> p i e", i=CI)
    edge_rows = sb("edge_rows", [G, 2, ROW], F32)
    edge_halves = edge_rows[:, :, :].rearrange("p b w -> p (b w)").bitcast(F16).rearrange("p (b w) -> p b w", b=2)
    slots_left = sb("slots_left", [G, EC], F32)
    codes = sb("codes", [G, 2, EC], F16)
    tabs = sb("tabs", [EC, 2, 3, G, 2], F16)
    chunk_of = sb("chunk_of", [G, NG], U32)
    chunk_col = sb("chunk_col", [G, 2, 1], U32)
    slot_top = sb("slot_top", [G, NG], F32)
    slot_max = sb("slot_max", [G, 1], F32)
    node_of = sb("node_of", [G, NG, WIN], U32)
    node_col = sb("node_col", [G, 2, WIN], U32)
    node_base = sb("node_base", [G, NG], F32)
    slot_oh = sb("slot_oh", [EC, WIN, G], F16)
    deg_scan = sb("deg_scan", [WIN, 2, G], F32)
    deg_max = sb("deg_max", [G, WIN], F32)
    deg_inv = sb("deg_inv", [G, NG, WIN], F32)
    sums = sb("sums", [D, 2, NCOL], F32)
    rows = sb("rows", [G, 2, WIN, D], F32)
    wm_t = sb("wm_t", [D, D], F32)
    ws_t = sb("ws_t", [D, D], F32)
    w_in = sb("w_in", [D, 2, D], F32)
    b_bc = sb("b_bc", [NP, D], F32)
    gamma_bc = sb("gamma_bc", [NP, D], F32)
    beta_bc = sb("beta_bc", [NP, D], F32)
    zero_row = sb("zero_row", [NP, D], F32)
    stats = sb("stats", [NP, BT, 6], F32)
    mv = sb("mv", [NP, NT, 2], F32)
    std = sb("std", [NP, NT], F32)
    rstd = sb("rstd", [NP, NT], F32)
    shift = sb("shift", [NP, NT], F32)
    h_t = sb("h_t", [D, 2, 4, NP], F32)
    diff = sb("diff", [128, 128], F32)
    ident = sb("ident", [128, 128], F32)
    ident16 = sb("ident16", [G, G], F16)
    tri_lt = sb("tri_lt", [CP, CP], F32)
    tri_le = sb("tri_le", [G, G], F32)
    ones = sb("ones", [128, 128], F32)
    iota_part = sb("iota_part", [EC, 128], F16)
    iota_cell = sb("iota_cell", [EC, MC], F16)
    iota_g = sb("iota_g", [CP, G], F32)
    step_no = sb("step_no", [G, NG], F32)
    next_step = sb("next_step", [G, G], F32)
    next_group = sb("next_group", [G, G], F32)
    cell_src = sb("cell_src", [EC, MC], F32)
    slot_sel = sb("slot_sel", [EC, WIN, WIN], F16)
    slot_src = sb("slot_src", [EC, WIN, WIN], F32)
    before_last = sb("before_last", [CP, 1], I32)
    ends_f = sb("ends_f", [CP, 3, CI], F32)
    wins = sb("wins", [CP, 3, CI], F32)
    n_steps = sb("n_steps", [CP, CI], F32)
    steps_inc = sb("steps_inc", [CP, CI], F32)
    steps_before = sb("steps_before", [CP, 1], F32)
    start = sb("start", [CP, CI], F32)
    start_gf = sb("start_gf", [CP, CI], F32)
    start_g = sb("start_g", [CP, CI], F32)
    start_k = sb("start_k", [CP, CI], F32)
    jump = sb("jump", [CP, CI], F32)
    jump_f = sb("jump_f", [CP, CI], F32)
    jump_hi = sb("jump_hi", [CP, CI], F32)
    jump_lo = sb("jump_lo", [CP, CI], F32)
    start_k2 = sb("start_k2", [CP, CI, 2], F16)
    iota_k = sb("iota_k", [CP, G], F16)
    marks = sb("marks", [G, 2, NG], F32)
    marks_lo = sb("marks_lo", [G, NG], F32)
    tot_scan = sb("tot_scan", [G, 2, NG], F32)
    tot_ex = sb("tot_ex", [G, 2, NG], F32)
    prefix = sb("prefix", [G, 2, NG], F32)
    window = sb("window", [G, NG], F32)
    cont = sb("cont", [G, NG], F32)
    cont_t = sb("cont_t", [NG, G], F32)
    cont_skip = sb("cont_skip", [G, NG + 1], F32)

    p_cnt = ps("p_cnt", [128, CB, 512])
    p_main = ps("p_main", [128, 2, 512])
    p_misc = ps("p_misc", [128, 512])
    p_degs = ps("p_degs", [128, 512])
    p_rows = ps("p_rows", [128, 4, D])
    p_tabs = p_misc[0:EC, 0:192].bitcast(F16).rearrange("p (c k) -> p c k", c=3)[:, :, 0:G]
    p_deg = p_degs[0:WIN, 0:G]
    p_degr = p_degs[0:G, 384:384 + WIN]

    x_landed = [sem(f"x_landed{b}") for b in range(NB)]
    w_landed = sem("w_landed")
    vec_landed = sem("vec_landed")
    before_landed = sem("before_landed")
    dst_landed = sem("dst_landed")
    src_landed = [sem("src_landed0"), sem("src_landed1")]
    parts_f = sem("parts_f")
    parts = sem("parts")
    src_scaled = sem("src_scaled")
    packed_dst = sem("packed_dst")
    packed_parts = sem("packed_parts")
    packed_tiles = sem("packed_tiles")
    chunks_stored = sem("chunks_stored")
    zeroed = sem("zeroed")
    zero_ready = sem("zero_ready")
    before_set = sem("before_set")
    padded = sem("padded")
    agg_padded = sem("agg_padded")
    iotas = sem("iotas")
    dve = sem("dve")
    consts_ready = sem("consts_ready")
    var_ready = sem("var_ready")
    std_ready = sem("std_ready")
    shift_ready = sem("shift_ready")
    scaled_x = sem("scaled_x")
    shifted_x = sem("shifted_x")
    h_ready = sem("h_ready")
    hi_ready = sem("hi_ready")
    lo_ready = sem("lo_ready")
    w_turned = sem("w_turned")
    w_ready = sem("w_ready")
    h_turned = sem("h_turned")
    ht_ready = sem("ht_ready")
    self_mm = sem("self_mm")
    self_ready = sem("self_ready")
    inc_ready = sem("inc_ready")
    before_mm = sem("before_mm")
    oh_steps = sem("oh_steps")
    marks_mm = sem("marks_mm")
    marks_ready = sem("marks_ready")
    prefix_mm = sem("prefix_mm")
    chunks_ready = sem("chunks_ready")
    windows_ready = sem("windows_ready")
    nodes_mm = sem("nodes_mm")
    nodes_ready = sem("nodes_ready")
    cont_ready = sem("cont_ready")
    cont_mm = sem("cont_mm")
    cont_turned = sem("cont_turned")
    cont_stored = sem("cont_stored")
    same_landed = sem("same_landed")
    gathered = [sem("gathered0"), sem("gathered1")]
    col_copied = sem("col_copied")
    pool_waits = sem("pool_waits")
    left_ready = sem("left_ready")
    slots_ready = sem("slots_ready")
    codes_ready = sem("codes_ready")
    tabs_mm = sem("tabs_mm")
    tabs_ready = sem("tabs_ready")
    onehots_ready = sem("onehots_ready")
    counts_mm = sem("counts_mm")
    slab_written = sem("slab_written")
    main_mm = sem("main_mm")
    sums_ready = sem("sums_ready")
    slot_ready = sem("slot_ready")
    deg_mm = sem("deg_mm")
    deg_scanned = sem("deg_scanned")
    degr_mm = sem("degr_mm")
    deg_max_done = sem("deg_max_done")
    deg_ready = sem("deg_ready")
    rows_mm = sem("rows_mm")
    rows_ready = sem("rows_ready")
    node_copied = sem("node_copied")
    scattered = [sem("scattered0"), sem("scattered1")]
    agg_landed = [sem(f"agg_landed{b}") for b in range(len(last_blocks))]
    xb_ready = sem("xb_ready")
    o_ready = [sem(f"o_ready{b}") for b in range(len(last_blocks))]
    o_relu = sem("o_relu")
    normed = sem("normed")
    scaled = sem("scaled")
    out_ready = [sem(f"out_ready{b}") for b in range(len(last_blocks))]
    stored = sem("stored")

    chunk_src = src.rearrange("(p i e) -> p i e", i=CI, e=EC)
    rows_packed = chunk_rows.rearrange("(p i) w -> p i w", i=CI)

    def node_tiles(rows, t0, k):
        full = rows[0:FP * NT, :].rearrange("(p t) d -> p t d", t=NT)
        pieces = [(slice(0, FP), slice(t0, t0 + k), full[:, t0:t0 + k, :])]
        if t0 < RT:
            t1 = min(t0 + k, RT)
            pieces.append((slice(FP, NP), slice(t0, t1), rows[FP * NT + t0:FP * NT + t1, :].rearrange("(p t) d -> p t d", p=1)))
        return pieces

    chunk_dst = dst.rearrange("(p i e) -> p i e", i=CI, e=EC)

    self_batches = [(t, min(4, NT - t)) for t in range(0, NT, 4)]
    BATCHES = len(self_batches)
    SUMS_AT = 1
    FIRST_ADD_AT = 7
    FIRST_LN_AT = 9
    ROWS_AT = 2

    def turned_h(n):
        return (p_misc[:, :], p_cnt[:, 0, :])[n % 2]

    with nc.Block() as block:

        @block.sync
        def _(sp):
            with nc.allow_non_contiguous_dma(reason="one destination per partition"):
                sp.dma_start(before_last[1:CP, :], chunk_dst[0:CP - 1, CI - 1:CI, EC - 1]).then_inc(before_landed, 16)
            sp.dma_start(dst_in, chunk_dst).then_inc(dst_landed, 16)
            for h in range(2):
                i = slice(h * CH, (h + 1) * CH)
                sp.dma_start(src_in[:, i, :], chunk_src[:, i, :]).then_inc(src_landed[h], 16)

            def load_x(b):
                for p, t, part in node_tiles(x, b * BT, KB[b]):
                    sp.dma_start(x_f32[p, t, :], part).then_inc(x_landed[b], 16)

            def store_chunks(h):
                i = slice(h * CH, (h + 1) * CH)
                sp.wait_ge(packed_dst, h + 1)
                sp.wait_ge(packed_parts, h + 1)
                sp.wait_ge(packed_tiles, h + 1)
                sp.dma_start(rows_packed[:, i, :], packed[:, i, :]).then_inc(chunks_stored, 16)

            sp.wait_ge(padded, 1)
            load_x(0)
            load_x(1)
            store_chunks(0)
            store_chunks(1)
            load_x(2)
            sp.dma_start(w_in[:, 0, :], w_msg).then_inc(w_landed, 16)
            sp.dma_start(w_in[:, 1, :], w_self).then_inc(w_landed, 16)
            sp.wait_ge(cont_turned, 1)
            sp.dma_start(cont_rows, cont_t[:, :]).then_inc(cont_stored, 16)
            sp.wait_ge(gathered[0], 16)
            sp.wait_ge(gathered[1], 16)
            load_x(3)
            load_x(4)
            sp.wait_ge(cont_stored, 16)
            sp.dma_start(same_win[:, :], cont_rows.rearrange("(a g) k -> a (g k)", a=1).to_broadcast([128, NG * G])).then_inc(same_landed, 16)
            sp.dma_start(b_bc[:, :], b_self.rearrange("(a d) -> a d", a=1).to_broadcast([NP, D])).then_inc(vec_landed, 16)
            sp.dma_start(gamma_bc[:, :], gamma.rearrange("(a d) -> a d", a=1).to_broadcast([NP, D])).then_inc(vec_landed, 16)
            sp.dma_start(beta_bc[:, :], beta.rearrange("(a d) -> a d", a=1).to_broadcast([NP, D])).then_inc(vec_landed, 16)
            sp.wait_ge(zero_ready, 1)
            for p, t, part in node_tiles(agg_rows, 0, NT):
                sp.dma_start(part, zero_row[p, :].unsqueeze(1).to_broadcast([p.stop - p.start, t.stop - t.start, D])).then_inc(zeroed, 16)
            sp.wait_ge(scattered[0], 16 * WIN * NG // 2)
            sp.wait_ge(scattered[1], 16 * WIN * NG // 2)
            sp.wait_ge(agg_padded, 1)
            for b, (t0, k) in enumerate(last_blocks):
                for p, t, part in node_tiles(agg_rows, t0, k):
                    sp.dma_start(agg_in[p, t, :], part).then_inc(agg_landed[b], 16)
            for b, (t0, k) in enumerate(last_blocks):
                sp.wait_ge(out_ready[b], 1)
                for p, t, part in node_tiles(out, t0, k):
                    sp.dma_start(part, agg_in[p, t, :]).then_inc(stored, 16)
            sp.wait_ge(stored, 16 * LB + 16 * sum(t0 < RT for t0, _ in last_blocks))

        @block.gpsimd
        def _(gp):
            nc.gpsimd.memset(before_last[0:1, :], -WIN).then_inc(before_set, 1)
            nc.gpsimd.memset(zero_row[:, :], 0.0).then_inc(zero_ready, 1)
            nc.gpsimd.iota(diff[:, :], [[-1, 128]], base=0, channel_multiplier=1, allow_small_or_imprecise_dtypes=True).then_inc(iotas, 1)
            nc.gpsimd.iota(iota_g[:, :], [[1, G]], base=0, channel_multiplier=0, allow_small_or_imprecise_dtypes=True).then_inc(iotas, 1)
            nc.gpsimd.iota(step_no[:, :], [[G, NG]], base=0, channel_multiplier=1, allow_small_or_imprecise_dtypes=True).then_inc(iotas, 1)
            nc.gpsimd.iota(slot_src[:, :, :], [[1, WIN], [-1, WIN]], base=0, channel_multiplier=0, allow_small_or_imprecise_dtypes=True).then_inc(iotas, 1)
            nc.gpsimd.iota(iota_part[:, :], [[1, 128]], base=0, channel_multiplier=0, allow_small_or_imprecise_dtypes=True).then_inc(iotas, 1)
            nc.gpsimd.iota(cell_src[:, :].rearrange("p (t r) -> p t r", r=WIN), [[1, NT], [SLOT_STEP, WIN]], base=SLOT_STEP, channel_multiplier=0, allow_small_or_imprecise_dtypes=True).then_inc(iotas, 1)

            def await_count(sem, value):
                gp.wait_ge(sem, value)
                gp.sem_inc(pool_waits, 1)

            def gather(par, i):
                await_count(col_copied, i)
                gp.indirect_dma_start(out=edge_rows[:, par, :], out_offset=None, in_=chunk_rows,
                                      in_offset=bass.IndirectOffsetOnAxis(ap=chunk_col[:, par, :], axis=0),
                                      bounds_check=NCH - 1, oob_is_err=False).then_inc(gathered[par], 16)

            def copy_cols(par, col):
                gp.tensor_copy(chunk_col[:, par, :], chunk_of[:, col]).then_inc(col_copied, 1)

            def make_cells(par, n):
                await_count(slots_ready, n)
                gp.tensor_tensor(codes[:, 0, :], codes[:, 1, :], edge_halves[:, par, 3 * EC:4 * EC], ALU.add).then_inc(codes_ready, 1)

            def scatter(par, col, n_rows, n_copied, steps=G):
                if n_copied is not None:
                    await_count(scattered[par], n_copied)
                gp.tensor_copy(node_col[:, par, :], node_of[:, col, :]).then_inc(node_copied, 1)
                await_count(node_copied, n_rows)
                await_count(rows_ready, n_rows)
                for q in range(WIN):
                    gp.indirect_dma_start(out=agg_rows, out_offset=bass.IndirectOffsetOnAxis(ap=node_col[0:steps, par, q:q + 1], axis=0),
                                          in_=rows[0:steps, par, q, :], in_offset=None,
                                          bounds_check=N - 1, oob_is_err=False).then_inc(scattered[par], 16)

            def one(a):
                return bass.ds(a, 1)

            def group(g, i, par, fetch=True, code=True, store=True, first_store=False, steps=G):
                if fetch:
                    await_count(tabs_ready, g + 1)
                    copy_cols(par, one(g + 2))
                    gather(par, g + 3)
                if code:
                    make_cells(1 - par, g + 2)
                if store:
                    scatter(1 - par, g - 3, g - 2, None if first_store else 16 * WIN * (i - 2 + par), steps)

            gp.wait_ge(chunks_ready, 1)
            copy_cols(0, slice(0, 1))
            copy_cols(1, slice(1, 2))
            gp.wait_ge(chunks_stored, 32)
            gather(0, 1)
            gather(1, 2)
            make_cells(0, 1)

            def normalize(b):
                t = slice(b * BT, b * BT + KB[b])
                gp.wait_ge(shift_ready, b + 1)
                gp.tensor_tensor(h_f32[:, t, :], x_f32[:, t, :], rstd[:, t].unsqueeze(2).to_broadcast([NP, KB[b], D]), ALU.mult).then_inc(scaled_x, 1)
                gp.wait_ge(scaled_x, b - FIRST_POOL_LN + 1)
                gp.tensor_tensor(h_f32[:, t, :], h_f32[:, t, :], shift[:, t].unsqueeze(2).to_broadcast([NP, KB[b], D]), ALU.add).then_inc(shifted_x, 1)

            def low_part(b):
                t = slice(b * BT, b * BT + KB[b])
                gp.wait_ge(hi_ready, b + 1)
                gp.tensor_tensor(h_lo[:, t, :], h_f32[:, t, :], h_hi[:, t, :], ALU.subtract).then_inc(lo_ready, 1)

            def add_beta(b):
                t = slice(b * BT, b * BT + KB[b])
                gp.wait_ge(h_ready, b * BT + KB[b])
                gp.tensor_tensor(x_f32[:, t, :], x_f32[:, t, :], beta_bc[:, :].unsqueeze(1).to_broadcast([NP, KB[b], D]), ALU.add).then_inc(xb_ready, 1)

            group(0, 0, 0, store=False)
            low_part(0)
            low_part(1)
            low_part(2)
            normalize(3)
            gp.wait_ge(nodes_ready, 1)
            gp.wait_ge(zeroed, 32)
            gp.wait_ge(vec_landed, 48)
            group(1, 0, 1, store=False)
            low_part(3)
            low_part(4)
            group(2, 1, 0, store=False)
            add_beta(0)
            add_beta(1)
            group(3, 1, 1, first_store=True)
            add_beta(2)
            group(4, 2, 0, first_store=True)
            add_beta(3)
            group(5, 2, 1)
            add_beta(4)
            with gp.Fori(3, NG // 2 - 1) as i:
                group(2 * i, i, 0)
                group(2 * i + 1, i, 1)
            group(NG - 2, NG // 2 - 1, 0, fetch=False)
            group(NG - 1, NG // 2 - 1, 1, fetch=False, code=False)
            for g in range(NG, NG + 3):
                if g == NG + 2:
                    gp.wait_ge(main_mm, NG)
                    gp.memset(agg_in[96:NP, RT:NT, :], 0.0).then_inc(agg_padded, 1)
                    gp.wait_ge(agg_padded, 1)
                group(g, g // 2, g % 2, fetch=False, code=False, steps=LG if g == NG + 2 else G)

            def add_self(b):
                t0, k = last_blocks[b]
                t = slice(t0, t0 + k)
                gp.wait_ge(agg_landed[b], 32 if t0 < RT else 16)
                gp.wait_ge(self_ready, -(-(t0 + k) // 4))
                gp.tensor_tensor(agg_in[:, t, :], agg_in[:, t, :], h_f32[:, t, :], ALU.add).then_inc(o_ready[b], 1)

            def add_x(b):
                t0, k = last_blocks[b]
                t = slice(t0, t0 + k)
                gp.wait_ge(scaled, b + 1)
                gp.tensor_tensor(agg_in[:, t, :], agg_in[:, t, :], x_f32[:, t, :], ALU.add).then_inc(out_ready[b], 1)

            gp.wait_ge(xb_ready, NB)
            for b in POOL_ADDS:
                add_self(b)
            for b in range(LB):
                if b not in DVE_OUT:
                    add_x(b)

        @block.scalar
        def _(act):
            def turn_codes(g, par=0):
                act.wait_ge(tabs_mm, g + 1)
                if not isinstance(g, int) or g >= 2:
                    act.wait_ge(onehots_ready, BPG * (g - 1))
                    act.wait_ge(slot_ready, g - 1)
                act.activation(tabs[:, par, :, :, :], p_tabs.unsqueeze(3).to_broadcast([EC, 3, G, 2]), ACT.Copy).then_inc(tabs_ready, 1)

            def make_slots(g, par):
                act.wait_ge(gathered[par], 16 if isinstance(g, int) and g == 0 else 8 * (g + 1 + (1 - par)))
                act.activation(slots_left[:, :], edge_rows[:, par, 0:EC], ACT.Relu, scale=-1.0, bias=slot_top[:, one(g)]).then_inc(left_ready, 1)
                act.wait_ge(left_ready, g + 1)
                act.activation(codes[:, 1, :], slots_left[:, :], ACT.Relu, scale=-1.0, bias=slot_max[:, :]).then_inc(slots_ready, 1)

            def one(a):
                return slice(a, a + 1) if isinstance(a, int) else bass.ds(a, 1)

            def first_std(b):
                t = slice(b * BT, b * BT + KB[b])
                act.wait_ge(var_ready, b + 1)
                act.activation(std[:, t], mv[:, t, 1], ACT.Sqrt, scale=HSCALE ** -2).then_inc(std_ready, 1)

            def tile_ln(b, j0, n):
                act.wait_ge(shift_ready, b + 1)
                for j in range(b * BT + j0, b * BT + j0 + n):
                    act.activation(h_f32[:, j, :], x_f32[:, j, :], ACT.Relu, scale=rstd[:, j:j + 1], bias=shift[:, j:j + 1]).then_inc(h_ready, 1)

            def high_part(b):
                t = slice(b * BT, b * BT + KB[b])
                act.wait_ge(h_ready, b * BT + KB[b])
                act.activation(h_hi[:, t, :], h_f32[:, t, :], ACT.Copy).then_inc(hi_ready, 1)

            def first_ln(b):
                first_std(b)
                tile_ln(b, 0, KB[b])
                high_part(b)

            act.wait_ge(dst_landed, 16)
            for h in range(2):
                i = slice(h * CH, (h + 1) * CH)
                act.activation(packed[:, i, 0:EC], dst_in[:, i, :], ACT.Copy).then_inc(packed_dst, 1)
            for h in range(2):
                i = slice(h * CH, (h + 1) * CH)
                act.wait_ge(src_landed[h], 16)
                act.activation(part_f[:, i, :], src_in[:, i, :], ACT.Copy, scale=1.0 / NT, bias=-(NT - 1) / 2.0 / NT).then_inc(parts_f, 1)
                act.wait_ge(parts_f, h + 1)
                act.activation(src_f[:, i, :], src_in[:, i, :], ACT.Copy, scale=1.0 / SLOT_STEP).then_inc(src_scaled, 1)
            for h in range(2):
                i = slice(h * CH, (h + 1) * CH)
                act.wait_ge(parts, h + 1)
                act.activation(packed_h[:, i, 0, :], part_r[:, i, :], ACT.Copy).then_inc(packed_parts, 1)

            def relu_x(b):
                t = slice(b * BT, b * BT + KB[b])
                act.wait_ge(shifted_x, b - FIRST_POOL_LN + 1)
                act.activation(h_f32[:, t, :], h_f32[:, t, :], ACT.Relu).then_inc(h_ready, KB[b])

            first_std(0)
            act.wait_ge(windows_ready, 1)
            make_slots(0, 0)
            tile_ln(0, 0, 3)
            turn_codes(0)
            tile_ln(0, 3, BT - 3)
            high_part(0)
            act.wait_ge(w_turned, 1)
            act.activation(wm_t[:, :], p_rows[:, 0, :], ACT.Copy, scale=1.0 / HSCALE).then_inc(w_ready, 1)
            act.activation(ws_t[:, :], p_rows[:, 1, :], ACT.Copy, scale=1.0 / HSCALE).then_inc(w_ready, 1)
            first_ln(1)

            def filler(g, u):
                if g == 0 and u == 1:
                    first_std(2)
                if g == 0 and 4 <= u < 9:
                    tile_ln(2, 2 * (u - 4), 2)
                if g == 0 and u == 5:
                    first_std(3)
                if g == 0 and u == 9:
                    high_part(2)
                    first_std(4)
                if g == 0 and u == 20:
                    relu_x(3)
                    high_part(3)
                if g == 1 and u < KB[4]:
                    tile_ln(4, u, 1)
                if g == 1 and u == KB[4]:
                    high_part(4)

            def group(g, par, counts=True, codes_next=True, has_rows=True, guard_rows=True, units=UPG, steps=G):
                rows_at = 19 if units == UPG else units - 1
                for u in range(units):
                    if counts:
                        act.wait_ge(counts_mm, UPG * g + u + 1)
                        if u == 0 and (not isinstance(g, int) or g >= 2):
                            act.wait_ge(main_mm, g - 1)
                        act.activation(slab[:, par, :, u * US * WIN:(u + 1) * US * WIN],
                                       p_cnt[:, u % CB, 0:US * MC].rearrange("p (t c) -> p t c", t=NT), ACT.Copy).then_inc(slab_written, 1)
                    if u == 2 and codes_next:
                        make_slots(g + 1, 1 - par)
                    if isinstance(g, int) and g < 2:
                        filler(g, u)
                    if u == 13 and codes_next:
                        turn_codes(g + 1, 1 - par)
                    if u == rows_at and has_rows:
                        act.wait_ge(rows_mm, g - 1)
                        act.wait_ge(deg_ready, g - 1)
                        if guard_rows:
                            act.wait_ge(scattered[par], 8 * WIN * (g - par) - 16 * WIN)
                        for q in range(WIN):
                            last = act.activation(rows[0:steps, par, q, :], p_rows[0:steps, q, :], ACT.Copy, scale=deg_inv[0:steps, g - 2, q:q + 1])
                        last.then_inc(rows_ready, 1)

            group(0, 0, has_rows=False)
            group(1, 1, has_rows=False)
            group(2, 0, guard_rows=False)
            group(3, 1, guard_rows=False)
            with act.Fori(2, NG // 2 - 1) as i:
                group(2 * i, 0)
                group(2 * i + 1, 1)
            group(NG - 2, 0)
            group(NG - 1, 1, codes_next=False, units=LU)

            def relu(b):
                t0, k = last_blocks[b]
                t = slice(t0, t0 + k)
                act.wait_ge(o_ready[b], 1)
                act.activation(agg_in[:, t, :], agg_in[:, t, :], ACT.Relu).then_inc(o_relu, 1)

            def last_std(b):
                t0, k = last_blocks[b]
                t = slice(t0, t0 + k)
                act.wait_ge(var_ready, NB + b + 1)
                act.activation(std[:, t], mv[:, t, 1], ACT.Sqrt).then_inc(std_ready, 1)

            for n, (t, k) in enumerate(self_batches):
                act.wait_ge(h_turned, n + 1)
                if n >= 2:
                    act.wait_ge(self_mm, n - 1)
                act.activation(h_t[:, n % 2, 0:k, :], turned_h(n).rearrange("p (t e) -> p t e", t=4)[:, 0:k, 0:NP], ACT.Copy).then_inc(ht_ready, 1)
                if n == 0:
                    group(NG, 0, counts=False, codes_next=False)
                if n == ROWS_AT:
                    group(NG + 1, 1, counts=False, codes_next=False, steps=LG)
                if n == FIRST_LN_AT:
                    relu(0)
                if n == FIRST_LN_AT + 2:
                    last_std(0)

            for b, (t0, k) in enumerate(last_blocks):
                if b:
                    last_std(b)
                if b + 1 < LB:
                    relu(b + 1)
                act.wait_ge(shift_ready, NB + b + 1)
                for j in range(t0, t0 + k):
                    last = act.activation(agg_in[:, j, :], agg_in[:, j, :], ACT.Identity, scale=rstd[:, j:j + 1], bias=shift[:, j:j + 1])
                last.then_inc(normed, 1)

        @block.vector
        def _(v):
            done = [0]

            def own(ins):
                done[0] += 1
                ins.then_inc(dve, 1)
                v.wait_ge(dve, done[0])

            def bn_of(tiles, t0, k=BT):
                for j in range(k):
                    last = v.bn_stats(stats[:, j, :], tiles[:, t0 + j, :])
                own(last)

            def aggr_of(t0, k=BT):
                for j in range(k):
                    last = v.bn_aggr(mv[:, t0 + j, :], stats[:, j, :])
                own(last)
                v.tensor_scalar(mv[:, t0:t0 + k, 1], mv[:, t0:t0 + k, 1], EPS, None, ALU.add).then_inc(var_ready, 1)

            def stats_of(tiles, t0, k=BT):
                bn_of(tiles, t0, k)
                aggr_of(t0, k)

            def first_stats(b):
                v.wait_ge(x_landed[b], 32 if b * BT < RT else 16)
                stats_of(x_f32, b * BT, KB[b])

            def shifts_of(n, t0, k=BT):
                t = slice(t0, t0 + k)
                v.wait_ge(std_ready, n + 1)
                own(v.reciprocal(rstd[:, t], std[:, t]))
                v.scalar_tensor_tensor(out=shift[:, t], in0=mv[:, t, 0], scalar=-1.0, in1=rstd[:, t], op0=ALU.mult, op1=ALU.mult).then_inc(shift_ready, 1)

            v.memset(x_f32[96:NP, RT:NT, :], 0.0).then_inc(padded, 1)
            v.wait_ge(iotas, 6)
            v.tensor_copy(iota_k[:, :], iota_g[:, :])
            v.tensor_scalar(ident[:, :], diff[:, :], 0.0, None, ALU.is_equal)
            v.tensor_scalar(ident16[:, :], diff[0:G, 0:G], 0.0, None, ALU.is_equal)
            v.tensor_scalar(tri_lt[:, :], diff[0:CP, 0:CP], 0.0, None, ALU.is_lt)
            v.tensor_scalar(tri_le[:, :], diff[0:G, 0:G], 0.0, None, ALU.is_le)
            v.tensor_scalar(next_step[:, :], diff[0:G, 0:G], 1.0, None, ALU.is_equal)
            v.tensor_scalar(next_group[:, :], diff[0:G, 0:G], float(1 - G), None, ALU.is_equal)
            v.tensor_scalar(slot_sel[:, :, :], slot_src[:, :, :], 0.0, None, ALU.is_equal)
            v.tensor_scalar(iota_cell[:, :], cell_src[:, :], 1.0 / SLOT_STEP, None, ALU.mult)
            v.memset(ones[:, :], 1.0)
            v.memset(slot_max[:, :], WIN + 1.0)
            v.memset(cont_skip[:, :], 0.0).then_inc(consts_ready, 1)

            v.wait_ge(before_landed, 16)
            v.wait_ge(before_set, 1)
            v.wait_ge(dst_landed, 16)
            half = ((WIN - 1) / 2.0, 1.0 / WIN, ALU.subtract, ALU.mult)
            v.tensor_scalar(ends_f[:, 0, :], dst_in[:, :, 0], *half)
            v.tensor_scalar(ends_f[:, 1, :], dst_in[:, :, EC - 1], *half)
            v.tensor_scalar(ends_f[:, 2, 1:CI], dst_in[:, 0:CI - 1, EC - 1], *half)
            own(v.tensor_scalar(ends_f[:, 2, 0:1], before_last[:, :], *half))
            own(v.tensor_scalar(wins[:, :, :], ends_f[:, :, :], MAGIC, MAGIC, ALU.add, ALU.subtract))
            own(v.scalar_tensor_tensor(out=n_steps[:, :], in0=wins[:, 1, :], scalar=1.0, in1=wins[:, 0, :], op0=ALU.add, op1=ALU.subtract))
            v.tensor_tensor_scan(steps_inc[:, :], ones[0:CP, 0:CI], n_steps[:, :], 0.0, ALU.mult, ALU.add).then_inc(inc_ready, 1)
            own(v.scalar_tensor_tensor(out=jump[:, :], in0=wins[:, 0, :], scalar=-1.0, in1=wins[:, 2, :], op0=ALU.add, op1=ALU.subtract))
            own(v.tensor_scalar(jump_f[:, :], jump[:, :], 1.0 / 64, MAGIC, ALU.mult, ALU.add))
            own(v.tensor_scalar(jump_hi[:, :], jump_f[:, :], MAGIC, None, ALU.subtract))
            v.scalar_tensor_tensor(out=jump_lo[:, :], in0=jump_hi[:, :], scalar=-64.0, in1=jump[:, :], op0=ALU.mult, op1=ALU.add)
            v.wait_ge(before_mm, 1)
            own(v.tensor_copy(steps_before[:, :], p_misc[0:CP, 0:1]))
            own(v.scalar_tensor_tensor(out=start[:, :], in0=steps_inc[:, :], scalar=steps_before[:, :], in1=n_steps[:, :], op0=ALU.add, op1=ALU.subtract))
            own(v.tensor_scalar(start_gf[:, :], start[:, :], (G - 1) / 2.0, 1.0 / G, ALU.subtract, ALU.mult))
            own(v.tensor_scalar(start_g[:, :], start_gf[:, :], MAGIC, MAGIC, ALU.add, ALU.subtract))
            own(v.scalar_tensor_tensor(out=start_k[:, :], in0=start_g[:, :], scalar=-float(G), in1=start[:, :], op0=ALU.mult, op1=ALU.add))
            own(v.tensor_copy(start_k2[:, :, :], start_k[:, :].unsqueeze(2).to_broadcast([CP, CI, 2])))

            def round_parts(h):
                i = slice(h * CH, (h + 1) * CH)
                v.wait_ge(parts_f, h + 1)
                v.tensor_scalar(part_r[:, i, :], part_f[:, i, :], MAGIC, MAGIC, ALU.add, ALU.subtract).then_inc(parts, 1)

            def pack_tiles(h):
                i = slice(h * CH, (h + 1) * CH)
                v.wait_ge(src_scaled, h + 1)
                v.wait_ge(parts, h + 1)
                v.scalar_tensor_tensor(out=packed_h[:, i, 1, :], in0=part_r[:, i, :], scalar=-float(NT) / SLOT_STEP, in1=src_f[:, i, :],
                                       op0=ALU.mult, op1=ALU.add).then_inc(packed_tiles, 1)

            round_parts(0)
            v.tensor_tensor(oh_k[:, :, :].rearrange("p i (c e) -> p i c e", e=2),
                            iota_k[:, :].rearrange("p (c e) -> p c e", e=2).unsqueeze(1).to_broadcast([CP, CI, G // 2, 2]),
                            start_k2[:, :, :].unsqueeze(2).to_broadcast([CP, CI, G // 2, 2]), ALU.is_equal)
            own(v.tensor_tensor(oh_g[:, :, 0, :], iota_g[:, 0:NG].unsqueeze(1).to_broadcast([CP, CI, NG]),
                                start_g[:, :].unsqueeze(2).to_broadcast([CP, CI, NG]), ALU.is_equal))
            v.tensor_tensor(oh_g[:, :, 1, :], oh_g[:, :, 0, :], jump_hi[:, :].unsqueeze(2).to_broadcast([CP, CI, NG]), ALU.mult)
            v.tensor_tensor(oh_g[:, :, 2, :], oh_g[:, :, 0, :], jump_lo[:, :].unsqueeze(2).to_broadcast([CP, CI, NG]), ALU.mult).then_inc(oh_steps, 1)
            pack_tiles(0)
            round_parts(1)
            pack_tiles(1)
            v.wait_ge(marks_mm, 1)
            v.tensor_copy(marks[:, 0, :], p_misc[0:G, 0:NG])
            own(v.tensor_copy(marks_lo[:, :], p_misc[0:G, 2 * NG:3 * NG]))
            v.scalar_tensor_tensor(out=marks[:, 1, :], in0=p_misc[0:G, NG:2 * NG], scalar=64.0, in1=marks_lo[:, :],
                                   op0=ALU.mult, op1=ALU.add).then_inc(marks_ready, 1)
            v.wait_ge(marks_ready, 1)
            v.tensor_scalar(cont[:, :], marks[:, 1, :], -1.0, None, ALU.is_equal).then_inc(cont_ready, 1)
            v.wait_ge(cont_ready, 1)
            v.wait_ge(consts_ready, 1)
            v.tensor_scalar(cont_skip[:, 0:NG], cont[:, :], SKIP, None, ALU.mult)
            v.wait_ge(prefix_mm, 1)
            totals = p_rows[0:G, 0, 0:2 * NG].rearrange("p (h g) -> p h g", h=2)
            within = p_rows[0:G, 1, 0:2 * NG].rearrange("p (h g) -> p h g", h=2)
            v.tensor_tensor_scan(tot_scan[:, 0, :], ones[0:G, 0:NG], totals[:, 0, :], 0.0, ALU.mult, ALU.add)
            own(v.tensor_tensor_scan(tot_scan[:, 1, :], ones[0:G, 0:NG], totals[:, 1, :], 0.0, ALU.mult, ALU.add))
            own(v.tensor_tensor(tot_ex[:, :, :], tot_scan[:, :, :], totals, ALU.subtract))
            own(v.tensor_tensor(prefix[:, :, :], tot_ex[:, :, :], within, ALU.add))
            v.tensor_scalar(chunk_of[:, :], prefix[:, 0, :], -1.0, None, ALU.add).then_inc(chunks_ready, 1)
            own(v.tensor_tensor(window[:, :], prefix[:, 1, :], step_no[:, :], ALU.add))
            v.tensor_scalar(slot_top[:, :], window[:, :], float(WIN), float(WIN), ALU.mult, ALU.add).then_inc(windows_ready, 1)
            v.wait_ge(cont_mm, 1)
            v.tensor_copy(cont_t[:, :], p_degs[0:NG, 0:G]).then_inc(cont_turned, 1)
            v.wait_ge(nodes_mm, 1)
            own(v.scalar_tensor_tensor(out=node_base[:, :], in0=window[:, :], scalar=float(WIN), in1=p_misc[0:G, 0:NG], op0=ALU.mult, op1=ALU.add))
            for r in range(WIN):
                last = v.tensor_scalar(node_of[:, :, r], node_base[:, :], float(r), None, ALU.add)
            last.then_inc(nodes_ready, 1)

            first_stats(0)
            shifts_of(0, 0)
            first_stats(1)

            def filler(n):
                if n == 0:
                    shifts_of(1, BT)
                    first_stats(2)
                if n == 1:
                    shifts_of(2, 2 * BT)
                    first_stats(3)
                if n == 2:
                    shifts_of(3, 3 * BT)
                    first_stats(4)
                if n == 4:
                    shifts_of(4, 4 * BT, KB[4])

            def group(g, par, build=True, join=True, first_join=False, units=UPG, width=G):
                if build:
                    v.wait_ge(tabs_ready, g + 1)
                scan_at, max_at, inv_at, join_at = (12, 16, 20, 16) if units == UPG else (4, units - 1, units - 1, 5)
                for u in range(units):
                    if build and u % UPB == 0:
                        n = u // UPB
                        r = n % RING
                        if not (isinstance(g, int) and g == 0 and n < RING):
                            v.wait_ge(counts_mm, UPG * g + u + UPB * (1 - RING))
                        bs = min(BS, (units - u) * US)
                        k = slice(u * US, u * US + bs)
                        if u == 0:
                            if not (isinstance(g, int) and g == 0):
                                v.wait_ge(deg_mm, g)
                            for q in range(WIN):
                                last = v.tensor_scalar(slot_oh[:, q, :], tabs[:, par, 2, :, 0], q + 1.0, None, ALU.is_equal)
                            last.then_inc(slot_ready, 1)
                        v.tensor_tensor(oh_part[:, r, 0:bs, :].rearrange("p s (c e) -> p s c e", e=2),
                                        iota_part[:, :].rearrange("p (c e) -> p c e", e=2).unsqueeze(1).to_broadcast([EC, bs, 64, 2]),
                                        tabs[:, par, 0, k, :].unsqueeze(2).to_broadcast([EC, bs, 64, 2]), ALU.is_equal)
                        v.tensor_tensor(oh_cell[:, r, 0:bs, :].rearrange("p s (c e) -> p s c e", e=2),
                                        iota_cell[:, :].rearrange("p (c e) -> p c e", e=2).unsqueeze(1).to_broadcast([EC, bs, MC // 2, 2]),
                                        tabs[:, par, 1, k, :].unsqueeze(2).to_broadcast([EC, bs, MC // 2, 2]), ALU.is_equal).then_inc(onehots_ready, 1)
                    if isinstance(g, int) and g == 0 and u % UPB == 0:
                        filler(u // UPB)
                    if build and u == scan_at:
                        v.wait_ge(deg_mm, g + 1)
                        first = isinstance(g, int) and g == 0
                        if first:
                            v.wait_ge(same_landed, 16)
                        if not first:
                            v.wait_ge(deg_scanned, g)
                        if not (isinstance(g, int) and g <= 1):
                            v.wait_ge(degr_mm, g - 1)
                        v.tensor_tensor_scan(deg_scan[:, par, :], same_win[0:WIN, at(g)], p_deg,
                                             0.0 if first else deg_scan[:, 1 - par, G - 1:G], ALU.mult, ALU.add).then_inc(deg_scanned, 1)
                    if u == join_at and join:
                        v.wait_ge(main_mm, g - 1)
                        if not first_join:
                            v.wait_ge(sums_ready, g - 2)
                            if not (isinstance(g, int) and g == 3):
                                v.wait_ge(rows_mm, g - 3)
                        for r4 in range(WIN):
                            c = slice(r4, width * WIN, WIN)
                            last = v.tensor_tensor_scan(sums[:, par, c], same_win[:, bass.ds((g - 2) * G, width)], p_main[:, par, c],
                                                        0.0 if first_join else sums[:, 1 - par, NCOL - WIN + r4:NCOL - WIN + r4 + 1],
                                                        ALU.mult, ALU.add)
                        last.then_inc(sums_ready, 1)
                    if build and u == max_at:
                        v.wait_ge(degr_mm, g + 1)
                        if not (isinstance(g, int) and g == 0):
                            v.wait_ge(deg_ready, g)
                        v.tensor_scalar(deg_max[:, :], p_degr, 1.0, None, ALU.max).then_inc(deg_max_done, 1)
                    if build and u == inv_at:
                        v.wait_ge(deg_max_done, g + 1)
                        v.reciprocal(deg_inv[:, g, :], deg_max[:, :]).then_inc(deg_ready, 1)

            def at(g):
                return bass.ds(g * G, G)

            group(0, 0, join=False)
            group(1, 1, join=False)
            group(2, 0, first_join=True)
            group(3, 1)
            with v.Fori(2, NG // 2 - 1) as i:
                group(2 * i, 0)
                group(2 * i + 1, 1)
            group(NG - 2, 0)
            group(NG - 1, 1, units=LU)
            group(NG, 0, build=False)

            def add_bias(n):
                t, k = self_batches[n]
                v.wait_ge(self_mm, n + 1)
                v.tensor_tensor(h_f32[:, t:t + k, :], p_cnt[0:NP, 1 + n % 2, 0:k * D].rearrange("p (t d) -> p t d", d=D),
                                b_bc[:, :].unsqueeze(1).to_broadcast([NP, k, D]), ALU.add).then_inc(self_ready, 1)

            def add_self(b):
                t0, k = last_blocks[b]
                t = slice(t0, t0 + k)
                v.wait_ge(agg_landed[b], 32 if t0 < RT else 16)
                v.wait_ge(self_ready, -(-(t0 + k) // 4))
                v.tensor_tensor(agg_in[:, t, :], agg_in[:, t, :], h_f32[:, t, :], ALU.add).then_inc(o_ready[b], 1)

            v.wait_ge(vec_landed, 48)
            for n in range(BATCHES):
                if n == SUMS_AT:
                    group(NG + 1, 1, build=False, width=LG)
                add_bias(n)
                if n == FIRST_ADD_AT:
                    add_self(0)
                if n == FIRST_LN_AT:
                    v.wait_ge(o_relu, 1)
                    stats_of(agg_in, *last_blocks[0])
                if n == FIRST_LN_AT + 1:
                    shifts_of(NB, *last_blocks[0])

            def finish(b):
                t0, k = last_blocks[b]
                t = slice(t0, t0 + k)
                v.wait_ge(normed, b + 1)
                v.tensor_tensor(agg_in[:, t, :], agg_in[:, t, :], gamma_bc[:, :].unsqueeze(1).to_broadcast([NP, k, D]), ALU.mult).then_inc(scaled, 1)
                if b in DVE_OUT:
                    v.wait_ge(xb_ready, NB)
                    v.wait_ge(scaled, b + 1)
                    v.tensor_tensor(agg_in[:, t, :], agg_in[:, t, :], x_f32[:, t, :], ALU.add).then_inc(out_ready[b], 1)

            add_self(1)
            for b in range(1, LB):
                v.wait_ge(o_relu, b + 1)
                stats_of(agg_in, *last_blocks[b])
                if b >= 2:
                    finish(b - 2)
                shifts_of(NB + b, *last_blocks[b])
                if b + 2 < LB and b + 2 not in POOL_ADDS:
                    add_self(b + 2)
            finish(LB - 2)
            finish(LB - 1)

        @block.tensor
        def _(pe):
            pe.wait_ge(consts_ready, 1)
            pe.wait_ge(inc_ready, 1)
            pe.matmul(p_misc[0:CP, 0:1], tri_lt[:, :], steps_inc[:, CI - 1:CI], start=True, stop=True).then_inc(before_mm, 1)
            pe.wait_ge(oh_steps, 1)
            for i in range(CI):
                mm = pe.matmul(p_misc[0:G, 0:3 * NG], oh_k[:, i, :], oh_g[:, i, :, :].rearrange("p h g -> p (h g)"),
                               start=(i == 0), stop=(i == CI - 1))
            mm.then_inc(marks_mm, 1)
            pe.wait_ge(marks_ready, 1)
            flat = marks[:, :, :].rearrange("p h g -> p (h g)")
            pe.matmul(p_rows[0:G, 0, 0:2 * NG], ones[0:G, 0:G], flat, start=True, stop=True)
            pe.matmul(p_rows[0:G, 1, 0:2 * NG], tri_le[:, :], flat, start=True, stop=True).then_inc(prefix_mm, 1)
            pe.wait_ge(windows_ready, 1)
            pe.matmul(p_misc[0:G, 0:NG], next_step[:, :], cont_skip[:, 0:NG], start=True, stop=False)
            pe.matmul(p_misc[0:G, 0:NG], next_group[:, :], cont_skip[:, 1:NG + 1], start=False, stop=True).then_inc(nodes_mm, 1)
            pe.wait_ge(cont_ready, 1)
            pe.transpose(p_degs[0:NG, 0:G], cont[:, :], ident[0:G, 0:G]).then_inc(cont_mm, 1)
            pe.wait_ge(w_landed, 32)
            pe.wait_ge(windows_ready, 1)
            pe.transpose(p_rows[:, 0, :], w_in[:, 0, :], ident[:, :])
            pe.transpose(p_rows[:, 1, :], w_in[:, 1, :], ident[:, :]).then_inc(w_turned, 1)

            def turn(g, par=0):
                pe.wait_ge(codes_ready, g + 1)
                if not (isinstance(g, int) and g == 0):
                    pe.wait_ge(tabs_ready, g)
                pe.transpose(p_tabs[:, 0, :], edge_halves[:, par, 2 * EC:3 * EC], ident16[:, :])
                for c in range(2):
                    mm = pe.transpose(p_tabs[:, 1 + c, :], codes[:, c, :], ident16[:, :])
                mm.then_inc(tabs_mm, 1)

            pe.wait_ge(nodes_ready, 1)
            turn(0)

            def counts(g, par, u):
                if u % UPB == 0:
                    pe.wait_ge(onehots_ready, BPG * g + u // UPB + 1)
                if not (isinstance(g, int) and g == 0 and u < CB):
                    pe.wait_ge(slab_written, UPG * g + u + 1 - CB)
                for s in range(US):
                    k = u % UPB * US + s
                    o = p_cnt[:, u % CB, 0:US * MC].rearrange("p (t s r) -> p t s r", s=US, r=WIN)[:, :, s, :]
                    mm = pe.matmul(o, oh_part[:, u // UPB % RING, k, :], oh_cell[:, u // UPB % RING, k, :].rearrange("p (t r) -> p t r", r=WIN),
                                   start=(s == 0), stop=(s == US - 1), skip_group_check=True)
                mm.then_inc(counts_mm, 1)

            def products(par, a0, a1, first, cols=NCOL):
                for m in range(a0, a1):
                    a, part = m // 2, m % 2
                    if first and m % (2 * BT) == 0:
                        pe.wait_ge(lo_ready, a // BT + 1)
                    mm = pe.matmul(p_main[:, par, 0:cols], (h_hi, h_lo)[part][:, a, :], slab[0:NP, par, a, 0:cols],
                                   start=(m == 0), stop=(m == 2 * NT - 1))
                return mm

            def group(g, par, build=True, prod=True, free=True, has_rows=True, codes_next=True, wait_rows=True, units=UPG):
                nb = units - FREE_UNITS
                deg_at, degr_at, rows_at = (4, 13, 18) if units == UPG else (2, units - 2, units - 1)
                for u in range(units):
                    if build:
                        counts(g, par, u)
                    if prod and u >= FREE_UNITS:
                        if u == FREE_UNITS:
                            pe.wait_ge(slab_written, UPG * g)
                            if free:
                                pe.wait_ge(sums_ready, g - 2)
                        j = u - FREE_UNITS
                        mm = products(1 - par, 2 * NT * j // nb, 2 * NT * (j + 1) // nb, isinstance(g, int) and g == 1)
                        if u == units - 1:
                            mm.then_inc(main_mm, 1)
                    if u == 12 and codes_next:
                        turn(g + 1, 1 - par)
                    if u == deg_at and build:
                        pe.wait_ge(slot_ready, g + 1)
                        if not (isinstance(g, int) and g == 0):
                            pe.wait_ge(deg_max_done, g)
                        for r in range(WIN):
                            mm = pe.matmul(p_deg, slot_sel[:, r, :], slot_oh[:, r, :], start=(r == 0), stop=(r == WIN - 1))
                        mm.then_inc(deg_mm, 1)
                    if u == degr_at and build:
                        pe.wait_ge(deg_scanned, g + 1)
                        mm = pe.matmul(p_degr, deg_scan[:, par, :], ident[0:WIN, 0:WIN], start=True, stop=True)
                        mm.then_inc(degr_mm, 1)
                    if u == rows_at and has_rows:
                        rows_of(g, par, wait_rows)

            def rows_of(g, par, wait_rows=True, steps=G):
                pe.wait_ge(sums_ready, g - 1)
                if wait_rows:
                    pe.wait_ge(rows_ready, g - 2)
                for q in range(WIN):
                    mm = pe.matmul(p_rows[0:steps, q, :], sums[:, par, q:steps * WIN:WIN], wm_t[:, :], start=True, stop=True)
                mm.then_inc(rows_mm, 1)

            group(0, 0, prod=False, has_rows=False)
            group(1, 1, free=False, has_rows=False)
            group(2, 0, free=False, wait_rows=False)
            group(3, 1)
            with pe.Fori(2, NG // 2 - 1) as i:
                group(2 * i, 0)
                group(2 * i + 1, 1)
            group(NG - 2, 0)
            group(NG - 1, 1, codes_next=False, units=LU)

            pe.wait_ge(w_ready, 2)
            def turn_h(n):
                t, k = self_batches[n]
                if n >= 2:
                    pe.wait_ge(ht_ready, n - 1)
                for j in range(k):
                    mm = pe.transpose(turned_h(n)[:, j * 128:j * 128 + NP], h_f32[:, t + j, :], ident[0:NP, 0:NP])
                mm.then_inc(h_turned, 1)

            pe.wait_ge(slab_written, UPG * (NG - 1) + LU)
            turn_h(0)
            pe.wait_ge(sums_ready, NG - 2)
            products(1, 0, NT, False, LG * WIN)
            rows_of(NG, 0)
            products(1, NT, 2 * NT, False, LG * WIN).then_inc(main_mm, 1)
            for n, (t, k) in enumerate(self_batches):
                if n == ROWS_AT:
                    rows_of(NG + 1, 1, steps=LG)
                if n + 1 < BATCHES:
                    turn_h(n + 1)
                pe.wait_ge(ht_ready, n + 1)
                if n >= 2:
                    pe.wait_ge(self_ready, n - 1)
                for j in range(k):
                    o = p_cnt[0:NP, 1 + n % 2, j * D:(j + 1) * D]
                    mm = pe.matmul(o, h_t[:, n % 2, j, :], ws_t[:, :], start=True, stop=True)
                mm.then_inc(self_mm, 1)


_INS = ["x", "src", "dst", "L0_gnn_W_msg", "L0_gnn_W_self", "L0_gnn_b_self", "L0_gnn_gamma", "L0_gnn_beta"]


def kernel(**inputs):
    import concourse.bacc as bacc
    from concourse.bass_utils import run_bass_kernel_spmd

    nc = bacc.Bacc("TRN2", target_bir_lowering=False, num_devices=1)
    arrays, args = {}, []
    for name in _INS:
        a = np.ascontiguousarray(inputs[name])
        arrays[f"in_{name}"] = a
        args.append(nc.dram_tensor(f"in_{name}", a.shape, mybir.dt.from_np(a.dtype), kind="ExternalInput").ap())
    out = nc.dram_tensor("out", inputs["x"].shape, F32, kind="ExternalOutput").ap()
    build_layer(nc, *args, out)
    r = run_bass_kernel_spmd(nc, [arrays], core_ids=[0])
    return r.results[0]["out"]
```
